# Optimizing a Trainium2 kernel written in Bass

```python
import numpy as np
import jax
import jax.numpy as jnp

def _softmax(x, axis=-1):
    return jax.nn.softmax(x, axis=axis)

def _gelu(x):
    return jax.nn.gelu(x, approximate=True)

def _silu(x):
    return jax.nn.silu(x)

def _sigmoid(x):
    return jax.nn.sigmoid(x)

def _layernorm(x, axis=-1, eps=1e-05):
    m = jnp.mean(x, axis=axis, keepdims=True)
    v = jnp.var(x, axis=axis, keepdims=True)
    return (x - m) / jnp.sqrt(v + eps)

def _scatter_add(tgt, idx, src, axis=0):
    return tgt.at[idx].add(src)

def _segment_sum(src, seg, n):
    return jax.ops.segment_sum(src, seg, n)
kernel_name = 'mk_seq_preln_d1_jaxref_r4_3d0f44'

def setup_inputs(seed: int=0):
    np.random.seed(seed)
    _w = jnp.asarray

    def _L0_attn_setup():
        import jax, jax.numpy as jnp
        import numpy as np
        HIDDEN = 1024
        NUM_HEADS = 32
        HEAD_DIM = HIDDEN // NUM_HEADS

        def _fp8_roundtrip(x):
            return x.astype(jnp.float8_e4m3fn).astype(jnp.float32)
        key = jax.random.key(seed)
        ks = jax.random.split(key, 10)
        B, S = (2, 1024)
        hidden_states = jax.random.normal(ks[0], (B, S, HIDDEN), dtype=jnp.float32)
        scale = 0.02

        def lin(kw, kb):
            w = jax.random.normal(kw, (HIDDEN, HIDDEN), dtype=jnp.float32) * scale
            b = jax.random.normal(kb, (HIDDEN,), dtype=jnp.float32) * scale
            return (w, b)
        wq, bq = lin(ks[1], ks[2])
        wk, bk = lin(ks[3], ks[4])
        wv, bv = lin(ks[5], ks[6])
        wl, bl = lin(ks[7], ks[8])
        wq, bq = (_fp8_roundtrip(wq), _fp8_roundtrip(bq))
        wk, bk = (_fp8_roundtrip(wk), _fp8_roundtrip(bk))
        wv, bv = (_fp8_roundtrip(wv), _fp8_roundtrip(bv))
        return {'hidden_states': hidden_states, 'wq': wq, 'bq': bq, 'wk': wk, 'bk': bk, 'wv': wv, 'bv': bv, 'wl': wl, 'bl': bl}
    _L0_attn_in = _L0_attn_setup()

    def _L0_ffn_setup():
        import jax, jax.numpy as jnp
        import numpy as np
        B, S, D_IN, D_OUT = (2, 512, 1024, 1024)
        E, K, R = (8, 2, 16)
        SCALING = 32.0 / 16.0
        key = jax.random.key(seed)
        ks = jax.random.split(key, 6)
        x = jax.random.normal(ks[0], (B, S, D_IN), dtype=jnp.float32)
        gate_w = jax.random.normal(ks[1], (E, D_IN), dtype=jnp.float32) * 0.02
        base_w = jax.random.normal(ks[2], (D_OUT, D_IN), dtype=jnp.float32) * 0.02
        base_b = jax.random.normal(ks[3], (D_OUT,), dtype=jnp.float32) * 0.02
        lora_A = jax.random.normal(ks[4], (E, R, D_IN), dtype=jnp.float32) * 0.02
        lora_B = jax.random.normal(ks[5], (E, D_OUT, R), dtype=jnp.float32) * 0.02
        return {'x': x, 'gate_w': gate_w, 'base_w': base_w, 'base_b': base_b, 'lora_A': lora_A, 'lora_B': lora_B}
    _L0_ffn_in = _L0_ffn_setup()
    _d = {'L0_attn_hidden_states': _L0_attn_in['hidden_states'], 'L0_attn_wq': _L0_attn_in['wq'], 'L0_attn_bq': _L0_attn_in['bq'], 'L0_attn_wk': _L0_attn_in['wk'], 'L0_attn_bk': _L0_attn_in['bk'], 'L0_attn_wv': _L0_attn_in['wv'], 'L0_attn_bv': _L0_attn_in['bv'], 'L0_attn_wl': _L0_attn_in['wl'], 'L0_attn_bl': _L0_attn_in['bl'], 'L0_ffn_gate_w': _L0_ffn_in['gate_w'], 'L0_ffn_base_w': _L0_ffn_in['base_w'], 'L0_ffn_base_b': _L0_ffn_in['base_b'], 'L0_ffn_lora_A': _L0_ffn_in['lora_A'], 'L0_ffn_lora_B': _L0_ffn_in['lora_B']}
    _x0 = _d['L0_attn_hidden_states']
    _d['L0_attn_hidden_states'] = jax.random.normal(jax.random.fold_in(jax.random.key(seed), 1), (2, 2048, 1024), dtype=_x0.dtype)
    del _x0
    return _d

def reference(L0_attn_hidden_states, L0_attn_wq, L0_attn_bq, L0_attn_wk, L0_attn_bk, L0_attn_wv, L0_attn_bv, L0_attn_wl, L0_attn_bl, L0_ffn_gate_w, L0_ffn_base_w, L0_ffn_base_b, L0_ffn_lora_A, L0_ffn_lora_B):

    def _L0_attn_ref(hidden_states, wq, bq, wk, bk, wv, bv, wl, bl):
        import jax, jax.numpy as jnp
        import numpy as np
        HIDDEN = 1024
        NUM_HEADS = 32
        HEAD_DIM = HIDDEN // NUM_HEADS

        def _fp8_roundtrip(x):
            return x.astype(jnp.float8_e4m3fn).astype(jnp.float32)
        B, S, E = hidden_states.shape
        H, D = (NUM_HEADS, HEAD_DIM)
        q = (hidden_states @ wq.T + bq).reshape(B, S, H, D)
        k = (hidden_states @ wk.T + bk).reshape(B, S, H, D)
        v = (hidden_states @ wv.T + bv).reshape(B, S, H, D)
        latent = hidden_states @ wl.T + bl
        scores = jnp.einsum('bshd,bstd->bsht', q, k) / np.sqrt(D).astype(np.float32)
        probs = jax.nn.softmax(scores, axis=-1)
        context = jnp.einsum('bsht,bstd->bshd', probs, v).reshape(B, S, E)
        return context

    def _L0_ffn_ref(x, gate_w, base_w, base_b, lora_A, lora_B):
        import jax, jax.numpy as jnp
        import numpy as np
        B, S, D_IN, D_OUT = (2, 512, 1024, 1024)
        E, K, R = (8, 2, 16)
        SCALING = 32.0 / 16.0
        gate_logits = jnp.einsum('bsd,ed->bse', x, gate_w)
        weights, selected = jax.lax.top_k(gate_logits, K)
        weights = jax.nn.softmax(weights.astype(jnp.float32), axis=2).astype(x.dtype)
        result = jnp.einsum('bsd,od->bso', x, base_w) + base_b
        w_full = jnp.sum(jax.nn.one_hot(selected, E, dtype=x.dtype) * weights[..., None], axis=2)
        low = jnp.einsum('bsd,erd->ebsr', x, lora_A)
        lora_out = jnp.einsum('ebsr,eor,bse->bso', low, lora_B, w_full)
        result = result + SCALING * lora_out
        return result
    x = L0_attn_hidden_states
    x = x + _L0_attn_ref(_layernorm(x, axis=-1), L0_attn_wq, L0_attn_bq, L0_attn_wk, L0_attn_bk, L0_attn_wv, L0_attn_bv, L0_attn_wl, L0_attn_bl)
    x = x + _L0_ffn_ref(_layernorm(x, axis=-1), L0_ffn_gate_w, L0_ffn_base_w, L0_ffn_base_b, L0_ffn_lora_A, L0_ffn_lora_B)
    return x

_drawn_inputs = setup_inputs


def setup_inputs(seed=0):
    import zlib

    import numpy as np

    out = dict(_drawn_inputs(seed))
    spreads = {}
    factors = {'L0_attn_bq': 31.796, 'L0_attn_bk': 25.72, 'L0_attn_bv': 8.0, 'L0_ffn_base_b': 3.589}
    for name, (base, spread) in spreads.items():
        noise = np.random.default_rng([zlib.crc32(name.encode()), seed]).standard_normal(out[name].shape)
        drawn = base * np.exp(spread * noise) if base else spread * noise
        out[name] = jnp.asarray(drawn.astype(out[name].dtype))
    for name, factor in factors.items():
        out[name] = (out[name] * factor).astype(out[name].dtype)
    return out
```

```python
from contextlib import ExitStack

import concourse.bass as bass
from concourse import mybir

P = 128
QD = 32
NQ = P // QD
HID = 1024
HEADS = 32
HD = HID // HEADS
assert HD == QD and HEADS == QD
KC = HID // P
HALF = 512
NB = HID // HALF
EXPERTS = 8
RANK = 16
ER = EXPERTS * RANK
AG = ER + EXPERTS
LORA_SCALING = 32.0 / 16.0
LN_EPS = 1e-5
X_SCALE_EXP = 8
W_SCALE_EXP = 14
SCORE_SCALE = 1.0 / float(HD) ** 0.5

ALU = mybir.AluOpType
ACT = mybir.ActivationFunctionType
AX = mybir.AxisListType
F32 = mybir.dt.float32
F16 = mybir.dt.float16
I32 = mybir.dt.int32
U32 = mybir.dt.uint32
RMAX = bass.bass_isa.ReduceOp.max

GROUPS = ("k", "q", "v", "base")


def block_kernel(nc, x, wT, agT, lora_b, biases, out):
    T = x.shape[0] // P
    with ExitStack() as ctx:
        def sb(name, shape, dt=F32):
            return ctx.enter_context(nc.sbuf_tensor(name, shape, dt))

        def ps(name, shape, dt=F32):
            return ctx.enter_context(nc.psum_tensor(name, shape, dt))

        def sem(name):
            return ctx.enter_context(nc.semaphore(name))

        w_hi = {g: sb(f"w_hi_{g}", [P, KC, HID], F16) for g in GROUPS}
        w_lo = {g: sb(f"w_lo_{g}", [P, KC, HID], F16) for g in GROUPS}
        ag_hi = sb("ag_hi", [P, KC, AG], F16)
        ag_lo = sb("ag_lo", [P, KC, AG], F16)
        lora_up = sb("lora_up", [P, HID])
        bias = {g: sb(f"bias_{g}", [P, HID]) for g in GROUPS}
        ident = sb("ident", [P, P])
        expert_no = sb("expert_no", [P, EXPERTS])
        eps = sb("eps", [P, 1])
        pow_half = sb("pow_half", [P, 1])
        x_scale = sb("x_scale", [P, 1])
        NG = len(GROUPS) + 1
        w_chunk_max = sb("w_chunk_max", [P, NG, KC])
        w_part_max = sb("w_part_max", [P, NG])
        w_max = sb("w_max", [P, NG])
        w_clamped = sb("w_clamped", [P, NG])
        w_exp = sb("w_exp", [P, NG], I32)
        w_scale_bits = sb("w_scale_bits", [P, NG], I32)
        w_undo_bits = sb("w_undo_bits", [P, NG], I32)
        w_scale = w_scale_bits[:, :].bitcast(F32)
        w_undo = w_undo_bits[:, :].bitcast(F32)
        lora_scale0 = sb("lora_scale0", [P, 1])
        lora_scale = sb("lora_scale", [P, 1])

        block_diag_len = QD * P
        work = sb("work", [P, block_diag_len + 9 * HID])
        at = [0]

        def carve(n):
            at[0] += n
            return work[:, at[0] - n:at[0]]

        stage = work[:, 0:KC * HID].rearrange("p (k n) -> p k n", k=KC)
        ag_stage = work[:, KC * HID:KC * HID + KC * AG].rearrange("p (k n) -> p k n", k=KC)
        ld = carve(HID)
        xn = carve(HID)
        res = carve(HID)
        x1 = carve(HID)
        ev = carve(HID)
        kt = carve(HID)
        turned = carve(HID)
        soft = carve(HID)
        pt = carve(HID)
        y = kt
        diag = carve(block_diag_len).rearrange("p (t c) -> p t c", t=QD)
        x_hi = sb("x_hi", [P, KC, P], F16)
        x_lo = sb("x_lo", [P, KC, P], F16)
        x2_hi = sb("x2_hi", [P, KC, P], F16)
        x2_lo = sb("x2_lo", [P, KC, P], F16)
        low = sb("low", [P, ER])
        low_t = sb("low_t", [P, P])
        stats = sb("stats", [P, 2, 2, 6])
        mv = sb("mv", [P, 2, 2])
        var = sb("var", [P, 2])
        root_var = sb("root_var", [P, 2])
        rstd = sb("rstd", [P, 2])
        top = sb("top", [P, QD])
        den = sb("den", [P, QD])
        inv = sb("inv", [P, QD])
        logits = sb("logits", [P, EXPERTS])
        best = sb("best", [P, 8])
        best_at = sb("best_at", [P, 8], U32)
        best_no = sb("best_no", [P, 8])
        gap = sb("gap", [P, 1])
        e2 = sb("e2", [P, 1])
        e_sum = sb("e_sum", [P, 1])
        w1 = sb("w1", [P, 1])
        w2 = sb("w2", [P, 1])
        hot1 = sb("hot1", [P, EXPERTS])
        hot2 = sb("hot2", [P, EXPERTS])
        w_full = sb("w_full", [P, EXPERTS])

        acc = [ps(f"acc{i}", [P, HALF]) for i in range(3)]
        turn_ps = ps("turn_ps", [P, HID])
        attn_ps = ps("attn_ps", [P, HID])
        low_ps = ps("low_ps", [P, HALF])

        w_loaded = [sem(f"w_loaded{k}") for k in range(KC)]
        ag_loaded = sem("ag_loaded")
        const_loaded = sem("const_loaded")
        ident_zero = sem("ident_zero")
        consts_set = sem("consts_set")
        max_chunk = sem("max_chunk")
        max_part = sem("max_part")
        max_all = sem("max_all")
        scale_step = sem("scale_step")
        scale_ready = sem("scale_ready")
        w_hi_done = sem("w_hi_done")
        w_lo_done = sem("w_lo_done")
        diag_zero = sem("diag_zero")
        lora_scaled = sem("lora_scaled")

        ld_loaded = sem("ld_loaded")
        res_loaded = sem("res_loaded")
        y_stored = sem("y_stored")
        mv1 = sem("mv1")
        var1 = sem("var1")
        root1 = sem("root1")
        rstd1 = sem("rstd1")
        xn1_ready = sem("xn1_ready")
        xt_done = sem("xt_done")
        xhi_ready = sem("xhi_ready")
        xlo_ready = sem("xlo_ready")
        k_acc = sem("k_acc")
        q_acc = sem("q_acc")
        v_acc = sem("v_acc")
        k_biased = sem("k_biased")
        q_biased = sem("q_biased")
        v_biased = sem("v_biased")
        kt_ready = sem("kt_ready")
        qt_ready = sem("qt_ready")
        vt_ready = sem("vt_ready")
        qdiag_ready = sem("qdiag_ready")
        vdiag_ready = sem("vdiag_ready")
        scored = sem("scored")
        top_ready = sem("top_ready")
        shifted = sem("shifted")
        exped = sem("exped")
        den_ready = sem("den_ready")
        inv_ready = sem("inv_ready")
        prob_ready = sem("prob_ready")
        pt_ready = sem("pt_ready")
        ctx_acc = sem("ctx_acc")
        ctx_turned = sem("ctx_turned")
        x1_ready = sem("x1_ready")
        mv2 = sem("mv2")
        var2 = sem("var2")
        root2 = sem("root2")
        rstd2 = sem("rstd2")
        xn2_ready = sem("xn2_ready")
        x1_biased = sem("x1_biased")
        x2t_done = sem("x2t_done")
        x2hi_ready = sem("x2hi_ready")
        x2lo_ready = sem("x2lo_ready")
        ag_acc = sem("ag_acc")
        best_ready = sem("best_ready")
        best_found = sem("best_found")
        gap_ready = sem("gap_ready")
        e2_ready = sem("e2_ready")
        no_ready = sem("no_ready")
        e_summed = sem("e_summed")
        w1_ready = sem("w1_ready")
        w2_ready = sem("w2_ready")
        hots_ready = sem("hots_ready")
        full_ready = sem("full_ready")
        low_ready = sem("low_ready")
        low_turned = sem("low_turned")
        lowt_ready = sem("lowt_ready")
        base_acc = sem("base_acc")
        base_free = sem("base_free")

        block = ctx.enter_context(nc.Block())
        n_split = NG * KC

        def rows(ap, t):
            return ap[bass.ds(t * P, P), :]

        def pipeline(eng, step, tail):
            step(0, prev=False, nxt=True)
            with eng.Fori(1, T - 1) as t:
                step(t, prev=True, nxt=True)
            step(T - 1, prev=True, nxt=False)
            tail(T)

        @block.sync
        def _(sp):
            for j in range(len(GROUPS)):
                for k in range(KC):
                    if j:
                        sp.wait_ge(w_hi_done, (j - 1) * KC + k + 1)
                        sp.wait_ge(w_lo_done, (j - 1) * KC + k + 1)
                    sp.dma_start(stage[:, k, :], wT[j, k * P:(k + 1) * P, :]).then_inc(w_loaded[k], 16)
                if j == 0:
                    sp.dma_start(ag_stage, agT.rearrange("(k p) n -> p k n", p=P)).then_inc(ag_loaded, 16)
                    sp.dma_start(lora_up[:, :], lora_b).then_inc(const_loaded, 16)
                    for b, g in enumerate(GROUPS):
                        sp.dma_start(bias[g][:, :], biases[b:b + 1, :].to_broadcast([P, HID])).then_inc(
                            const_loaded, 16)
            sp.wait_ge(w_hi_done, n_split)
            sp.wait_ge(w_lo_done, n_split)
            sp.dma_start(ld, rows(x, 0)).then_inc(ld_loaded, 16)
            sp.dma_start(res, rows(x, 0)).then_inc(res_loaded, 16)

            def store(p):
                sp.wait_ge(base_free, 2 * p + 4)
                sp.dma_start(rows(out, p), y).then_inc(y_stored, 16)

            def step(t, prev, nxt):
                if nxt:
                    sp.wait_ge(xn1_ready, t + 1)
                    sp.dma_start(ld, rows(x, t + 1)).then_inc(ld_loaded, 16)
                if prev:
                    store(t - 1)
                if nxt:
                    sp.wait_ge(x1_ready, t + 1)
                    sp.dma_start(res, rows(x, t + 1)).then_inc(res_loaded, 16)

            pipeline(sp, step, lambda t: store(t - 1))
            sp.wait_ge(y_stored, 16 * T)

        @block.gpsimd
        def _(pool):
            nc.gpsimd.memset(ident[:, :], 0.0).then_inc(ident_zero, 1)
            pool.wait_ge(ident_zero, 1)
            nc.gpsimd.affine_select(out=ident[:, :], in_=ident[:, :], compare_op=ALU.not_equal, fill=1.0, base=0,
                                    pattern=[[-1, P]], channel_multiplier=1).then_inc(consts_set, 1)
            for e in range(EXPERTS):
                nc.gpsimd.memset(expert_no[:, e:e + 1], float(e)).then_inc(consts_set, 1)
            nc.gpsimd.memset(eps[:, :], LN_EPS).then_inc(consts_set, 1)
            nc.gpsimd.memset(pow_half[:, :], -0.5).then_inc(consts_set, 1)
            nc.gpsimd.memset(x_scale[:, :], 2.0 ** X_SCALE_EXP).then_inc(consts_set, 1)
            for j in range(NG):
                pool.wait_ge(max_part, j + 1)
                nc.gpsimd.partition_all_reduce(w_max[:, j:j + 1], w_part_max[:, j:j + 1], P, RMAX).then_inc(max_all, 1)

            pool.wait_ge(w_hi_done, n_split)
            pool.wait_ge(w_lo_done, n_split)
            nc.gpsimd.memset(diag, 0.0).then_inc(diag_zero, 1)
            pool.wait_ge(consts_set, EXPERTS + 4)

            def root(t, i, mv_ready, var_ready, root_ready, rstd_ready):
                pool.wait_ge(mv_ready, t + 1)
                nc.gpsimd.tensor_tensor(var[:, i:i + 1], mv[:, i, 1:2], eps[:, :], ALU.add).then_inc(var_ready, 1)
                pool.wait_ge(var_ready, t + 1)
                nc.gpsimd.tensor_tensor(root_var[:, i:i + 1], var[:, i:i + 1], pow_half[:, :],
                                        ALU.pow).then_inc(root_ready, 1)
                pool.wait_ge(root_ready, t + 1)
                nc.gpsimd.tensor_tensor(rstd[:, i:i + 1], root_var[:, i:i + 1], x_scale[:, :],
                                        ALU.mult).then_inc(rstd_ready, 1)

            root(0, 0, mv1, var1, root1, rstd1)
            pool.wait_ge(const_loaded, 16 * (len(GROUPS) + 1))

            def step(t, prev, nxt):
                if nxt:
                    root(t + 1, 0, mv1, var1, root1, rstd1)
                root(t, 1, mv2, var2, root2, rstd2)
                pool.wait_ge(xn2_ready, t + 1)
                nc.gpsimd.tensor_tensor(x1, x1, bias["base"][:, :], ALU.add).then_inc(x1_biased, 1)

            pipeline(pool, step, lambda t: None)

        @block.scalar
        def _(act):
            def split_hi(dst, src, j):
                nc.scalar.activation(dst, src, ACT.Copy, scale=w_scale[:, j:j + 1]).then_inc(w_hi_done, 1)

            for j, g in enumerate(GROUPS):
                act.wait_ge(scale_ready, j + 1)
                for k in range(KC):
                    split_hi(w_hi[g][:, k, :], stage[:, k, :], j)
            act.wait_ge(scale_ready, NG)
            for k in range(KC):
                split_hi(ag_hi[:, k, :], ag_stage[:, k, :], NG - 1)

            def rows_hi(t, dst, done, ready):
                for h in range(2):
                    act.wait_ge(done, 2 * t + h + 1)
                    c = KC // 2
                    nc.scalar.copy(dst[:, h * c:(h + 1) * c, :],
                                   turn_ps[:, h * HALF:(h + 1) * HALF].rearrange("p (k n) -> p k n", k=c)
                                   ).then_inc(ready, 1)

            def spread(ready):
                src = turned.rearrange("p (t c) -> p t c", t=QD)
                for g in range(NQ):
                    s = slice(g * QD, (g + 1) * QD)
                    nc.scalar.copy(diag[s, :, s], src[s, :, :]).then_inc(ready, 1)

            rows_hi(0, x_hi, xt_done, xhi_ready)
            act.wait_ge(diag_zero, 1)

            def gate_exp(p):
                act.wait_ge(gap_ready, p + 1)
                nc.scalar.activation(e2[:, :], gap[:, :], ACT.Exp).then_inc(e2_ready, 1)

            def low_copy(p):
                act.wait_ge(low_turned, p + 1)
                nc.scalar.copy(low_t[:, :], low_ps[:, 0:P]).then_inc(lowt_ready, 1)

            def dense_side(p):
                rows_hi(p, x2_hi, x2t_done, x2hi_ready)
                gate_exp(p)
                low_copy(p)

            def step(t, prev, nxt):
                if prev:
                    dense_side(t - 1)
                act.wait_ge(qt_ready, t + 1)
                if prev:
                    act.wait_ge(ctx_acc, t)
                spread(qdiag_ready)
                if nxt:
                    act.wait_ge(v_acc, 2 * t + 2)
                    rows_hi(t + 1, x_hi, xt_done, xhi_ready)
                act.wait_ge(shifted, t + 1)
                nc.scalar.activation(soft, soft, ACT.Exp, scale=SCORE_SCALE).then_inc(exped, 1)
                act.wait_ge(vt_ready, t + 1)
                act.wait_ge(scored, t + 1)
                spread(vdiag_ready)

            pipeline(act, step, lambda t: dense_side(t - 1))

        @block.vector
        def _(dve):
            nc.vector.memset(low[:, :], 0.0).then_inc(base_free, 2)

            def scales(j):
                dve.wait_ge(max_chunk, sum(chunks[:j + 1]))
                nc.vector.tensor_reduce(w_part_max[:, j:j + 1], w_chunk_max[:, j, 0:chunks[j]], AX.X,
                                        ALU.max).then_inc(max_part, 1)
                dve.wait_ge(max_all, j + 1)
                nc.vector.tensor_scalar(w_clamped[:, j:j + 1], w_max[:, j:j + 1], 2.0 ** -90, None,
                                        ALU.max).then_inc(scale_step, 1)
                dve.wait_ge(scale_step, 2 * j + 1)
                nc.vector.tensor_single_scalar(w_exp[:, j:j + 1], w_clamped[:, j:j + 1].bitcast(I32), 0x7F800000,
                                               ALU.bitwise_and).then_inc(scale_step, 1)
                dve.wait_ge(scale_step, 2 * j + 2)
                nc.vector.tensor_scalar(w_undo_bits[:, j:j + 1], w_exp[:, j:j + 1],
                                        float((W_SCALE_EXP + X_SCALE_EXP) << 23), None, ALU.subtract
                                        ).then_inc(undo_ready, 1)
                nc.vector.tensor_scalar(w_scale_bits[:, j:j + 1], w_exp[:, j:j + 1], -1.0,
                                        float((W_SCALE_EXP + 254) << 23), ALU.mult, ALU.add).then_inc(scale_ready, 1)

            undo_ready = sem("undo_ready")
            chunks = [KC] * len(GROUPS) + [1]

            def split_lo(dst, src, hi, j):
                nc.vector.scalar_tensor_tensor(out=dst, in0=src, scalar=w_scale[:, j:j + 1], in1=hi,
                                               op0=ALU.mult, op1=ALU.subtract).then_inc(w_lo_done, 1)

            for j, g in enumerate(GROUPS):
                for k in range(KC):
                    dve.wait_ge(w_loaded[k], 16 * (j + 1))
                    nc.vector.tensor_reduce(w_chunk_max[:, j, k:k + 1], stage[:, k, :], AX.X, ALU.max,
                                            apply_absolute_value=True).then_inc(max_chunk, 1)
                scales(j)
                if j == len(GROUPS) - 1:
                    dve.wait_ge(ag_loaded, 16)
                    nc.vector.tensor_reduce(w_chunk_max[:, NG - 1, 0:1], ag_stage, AX.XY, ALU.max,
                                            apply_absolute_value=True).then_inc(max_chunk, 1)
                    scales(NG - 1)
                for k in range(KC):
                    dve.wait_ge(w_hi_done, j * KC + k + 1)
                    dve.wait_ge(scale_ready, j + 1)
                    split_lo(w_lo[g][:, k, :], stage[:, k, :], w_hi[g][:, k, :], j)
            for k in range(KC):
                dve.wait_ge(w_hi_done, len(GROUPS) * KC + k + 1)
                split_lo(ag_lo[:, k, :], ag_stage[:, k, :], ag_hi[:, k, :], NG - 1)
            dve.wait_ge(undo_ready, NG)
            nc.vector.tensor_tensor(lora_scale0[:, :], w_undo[:, NG - 1:NG], w_scale[:, NG - 2:NG - 1],
                                    ALU.mult).then_inc(lora_scaled, 1)
            dve.wait_ge(lora_scaled, 1)
            nc.vector.tensor_scalar(lora_scale[:, :], lora_scale0[:, :], 2.0 ** X_SCALE_EXP * LORA_SCALING, None,
                                    ALU.mult).then_inc(lora_scaled, 1)
            dve.wait_ge(lora_scaled, 2)
            dve.wait_ge(const_loaded, 16 * (len(GROUPS) + 1))
            dve.wait_ge(consts_set, EXPERTS + 4)

            def ln_stats(i, src, mean_ready):
                for h in range(2):
                    nc.vector.bn_stats(stats[:, i, h, :], src[:, h * HALF:(h + 1) * HALF])
                dve.drain()
                nc.vector.bn_aggr(mv[:, i, :], stats[:, i, :, :].rearrange("p a b -> p (a b)")).then_inc(mean_ready, 1)

            def normalise(t, i, src, rstd_ready, ready):
                dve.wait_ge(rstd_ready, t + 1)
                nc.vector.tensor_scalar(xn, src, mv[:, i, 0:1], rstd[:, i:i + 1], ALU.subtract,
                                        ALU.mult).then_inc(ready, 1)

            def rows_lo(t, dst, hi, hi_ready, ready):
                c = KC // 2
                for h in range(2):
                    dve.wait_ge(hi_ready, 2 * t + h + 1)
                    nc.vector.tensor_tensor(dst[:, h * c:(h + 1) * c, :],
                                            turn_ps[:, h * HALF:(h + 1) * HALF].rearrange("p (k n) -> p k n", k=c),
                                            hi[:, h * c:(h + 1) * c, :], ALU.subtract).then_inc(ready, 1)

            def add_bias(t, n, g, j, bank, acc_done, biased):
                dve.wait_ge(acc_done, 2 * t + n + 1)
                s = slice(n * HALF, (n + 1) * HALF)
                nc.vector.scalar_tensor_tensor(out=ev[:, s], in0=acc[bank][:, :], scalar=w_undo[:, j:j + 1],
                                               in1=bias[g][:, s], op0=ALU.mult, op1=ALU.add).then_inc(biased, 1)

            ev_heads = ev.rearrange("p (h d) -> p h d", h=HEADS)

            dve.wait_ge(ld_loaded, 16)
            ln_stats(0, ld, mv1)
            normalise(0, 0, ld, rstd1, xn1_ready)
            rows_lo(0, x_lo, x_hi, xhi_ready, xlo_ready)

            def gating(p):
                dve.wait_ge(ag_acc, p + 1)
                nc.vector.tensor_scalar(logits[:, :], acc[0][:, ER:AG], w_undo[:, NG - 1:NG], None,
                                        ALU.mult)
                dve.drain()
                nc.vector.max(best[:, :], logits[:, :]).then_inc(best_ready, 1)
                dve.wait_ge(best_ready, p + 1)
                nc.vector.tensor_tensor(gap[:, :], best[:, 1:2], best[:, 0:1], ALU.subtract).then_inc(gap_ready, 1)
                nc.vector.max_index(best_at[:, :], best[:, :], logits[:, :]).then_inc(best_found, 1)
                dve.wait_ge(best_found, p + 1)
                nc.vector.tensor_copy(best_no[:, :], best_at[:, :]).then_inc(no_ready, 1)
                dve.wait_ge(e2_ready, p + 1)
                nc.vector.tensor_scalar(e_sum[:, :], e2[:, :], 1.0, None, ALU.add).then_inc(e_summed, 1)
                dve.wait_ge(e_summed, p + 1)
                nc.vector.reciprocal(w1[:, :], e_sum[:, :]).then_inc(w1_ready, 1)
                dve.wait_ge(w1_ready, p + 1)
                nc.vector.tensor_tensor(w2[:, :], e2[:, :], w1[:, :], ALU.mult).then_inc(w2_ready, 1)
                dve.wait_ge(no_ready, p + 1)
                nc.vector.tensor_scalar(hot1[:, :], expert_no[:, :], best_no[:, 0:1], w1[:, 0:1], ALU.is_equal,
                                        ALU.mult).then_inc(hots_ready, 1)
                dve.wait_ge(w2_ready, p + 1)
                nc.vector.tensor_scalar(hot2[:, :], expert_no[:, :], best_no[:, 1:2], w2[:, 0:1], ALU.is_equal,
                                        ALU.mult).then_inc(hots_ready, 1)
                dve.wait_ge(hots_ready, 2 * p + 2)
                nc.vector.tensor_tensor(w_full[:, :], hot1[:, :], hot2[:, :], ALU.add).then_inc(full_ready, 1)
                dve.wait_ge(full_ready, p + 1)
                nc.vector.scalar_tensor_tensor(
                    out=low[:, :].rearrange("p (e r) -> p e r", e=EXPERTS),
                    in0=acc[0][:, 0:ER].rearrange("p (e r) -> p e r", e=EXPERTS), scalar=lora_scale[:, 0:1],
                    in1=w_full[:, :].unsqueeze(2).to_broadcast([P, EXPERTS, RANK]),
                    op0=ALU.mult, op1=ALU.mult).then_inc(low_ready, 1)

            def finish(p, n):
                s = slice(n * HALF, (n + 1) * HALF)
                if n == 0:
                    dve.wait_ge(x1_biased, p + 1)
                dve.wait_ge(base_acc, 2 * p + n + 1)
                nc.vector.scalar_tensor_tensor(out=y[:, s], in0=acc[1 + n][:, :], scalar=w_undo[:, NG - 2:NG - 1],
                                               in1=x1[:, s], op0=ALU.mult, op1=ALU.add).then_inc(base_free, 1)

            def step(t, prev, nxt):
                add_bias(t, 0, "k", 0, 0, k_acc, k_biased)
                add_bias(t, 1, "k", 0, 1, k_acc, k_biased)
                if nxt:
                    dve.wait_ge(ld_loaded, 16 * (t + 2))
                    ln_stats(0, ld, mv1)
                dve.wait_ge(k_biased, 2 * t + 2)
                nc.vector.transpose(kt.rearrange("p (t h) -> p h t", t=QD), ev_heads).then_inc(kt_ready, 1)
                if prev:
                    rows_lo(t - 1, x2_lo, x2_hi, x2hi_ready, x2lo_ready)
                if nxt:
                    if prev:
                        dve.wait_ge(x2t_done, 2 * t)
                    normalise(t + 1, 0, ld, rstd1, xn1_ready)
                dve.wait_ge(kt_ready, t + 1)
                add_bias(t, 0, "q", 1, 2, q_acc, q_biased)
                if prev:
                    gating(t - 1)
                add_bias(t, 1, "q", 1, 1, q_acc, q_biased)
                dve.wait_ge(q_biased, 2 * t + 2)
                if prev:
                    dve.wait_ge(vdiag_ready, NQ * t)
                nc.vector.transpose(turned.rearrange("p (t h) -> p h t", t=QD), ev_heads).then_inc(qt_ready, 1)
                dve.wait_ge(qt_ready, t + 1)
                add_bias(t, 0, "v", 2, 2, v_acc, v_biased)
                add_bias(t, 1, "v", 2, 0, v_acc, v_biased)
                dve.wait_ge(v_biased, 2 * t + 2)
                dve.wait_ge(qdiag_ready, NQ * (t + 1))
                nc.vector.transpose(turned.rearrange("p (t d) -> p d t", t=QD),
                                    ev.rearrange("p (h d) -> p d h", h=HEADS)).then_inc(vt_ready, 1)
                if nxt:
                    dve.wait_ge(v_acc, 2 * t + 2)
                    rows_lo(t + 1, x_lo, x_hi, xhi_ready, xlo_ready)
                dve.wait_ge(scored, t + 1)
                scores = attn_ps[:, :].rearrange("p (t c) -> p t c", t=QD)
                s3 = soft.rearrange("p (t c) -> p t c", t=QD)
                nc.vector.tensor_reduce(top[:, :], scores, AX.X, ALU.max).then_inc(top_ready, 1)
                dve.wait_ge(top_ready, t + 1)
                if prev:
                    dve.wait_ge(pt_ready, t)
                nc.vector.tensor_tensor(s3, scores, top[:, :].unsqueeze(2).to_broadcast([P, QD, QD]),
                                        ALU.subtract).then_inc(shifted, 1)
                dve.wait_ge(exped, t + 1)
                nc.vector.tensor_reduce(den[:, :], s3, AX.X, ALU.add).then_inc(den_ready, 1)
                dve.wait_ge(den_ready, t + 1)
                nc.vector.reciprocal(inv[:, :], den[:, :]).then_inc(inv_ready, 1)
                dve.wait_ge(inv_ready, t + 1)
                nc.vector.tensor_tensor(s3, s3, inv[:, :].unsqueeze(2).to_broadcast([P, QD, QD]),
                                        ALU.mult).then_inc(prob_ready, 1)
                dve.wait_ge(prob_ready, t + 1)
                if prev:
                    dve.wait_ge(ctx_acc, t)
                nc.vector.transpose(pt, soft).then_inc(pt_ready, 1)
                if prev:
                    finish(t - 1, 0)
                    finish(t - 1, 1)
                dve.wait_ge(vt_ready, t + 1)
                dve.wait_ge(ctx_acc, t + 1)
                nc.vector.transpose(ev_heads, attn_ps[:, :].rearrange("p (t h) -> p h t", t=QD)
                                    ).then_inc(ctx_turned, 1)
                dve.wait_ge(ctx_turned, t + 1)
                dve.wait_ge(res_loaded, 16 * (t + 1))
                if prev:
                    dve.wait_ge(base_free, 2 * t + 2)
                nc.vector.tensor_tensor(x1, ev, res, ALU.add).then_inc(x1_ready, 1)
                dve.wait_ge(x1_ready, t + 1)
                ln_stats(1, x1, mv2)
                if nxt:
                    dve.wait_ge(xt_done, 2 * t + 4)
                normalise(t, 1, x1, rstd2, xn2_ready)
                if prev:
                    dve.wait_ge(y_stored, 16 * t)

            def tail(t):
                rows_lo(t - 1, x2_lo, x2_hi, x2hi_ready, x2lo_ready)
                gating(t - 1)
                finish(t - 1, 0)
                finish(t - 1, 1)

            pipeline(dve, step, tail)

        @block.tensor
        def _(pe):
            pe.wait_ge(consts_set, EXPERTS + 4)
            pe.wait_ge(w_hi_done, n_split)
            pe.wait_ge(w_lo_done, n_split)
            pe.wait_ge(const_loaded, 16 * (len(GROUPS) + 1))

            def turn_rows(t, xn_ready, done):
                pe.wait_ge(xn_ready, t + 1)
                for k in range(KC):
                    mm = nc.tensor.transpose(turn_ps[:, k * P:(k + 1) * P], xn[:, k * P:(k + 1) * P], ident[:, :])
                    if k % (KC // 2) == KC // 2 - 1:
                        mm.then_inc(done, 1)

            def product(dst, hi, lo, w_h, w_l, cols, more=False):
                for k in range(KC):
                    nc.tensor.matmul(dst, hi[:, k, :], w_h[:, k, cols], start=(k == 0), stop=False)
                    nc.tensor.matmul(dst, hi[:, k, :], w_l[:, k, cols], start=False, stop=False)
                    mm = nc.tensor.matmul(dst, lo[:, k, :], w_h[:, k, cols], start=False,
                                          stop=(k == KC - 1 and not more))
                return mm

            def project(g, n, bank, done):
                product(acc[bank][:, :], x_hi, x_lo, w_hi[g], w_lo[g],
                        slice(n * HALF, (n + 1) * HALF)).then_inc(done, 1)

            def experts(p):
                pe.wait_ge(x2hi_ready, 2 * p + 2)
                pe.wait_ge(x2lo_ready, 2 * p + 2)
                product(acc[0][:, 0:AG], x2_hi, x2_lo, ag_hi, ag_lo, slice(0, AG)).then_inc(ag_acc, 1)

            def turn_low(p):
                pe.wait_ge(low_ready, p + 1)
                nc.tensor.transpose(low_ps[:, 0:P], low[:, :], ident[:, :]).then_inc(low_turned, 1)

            def dense(p, n):
                s = slice(n * HALF, (n + 1) * HALF)
                product(acc[1 + n][:, :], x2_hi, x2_lo, w_hi["base"], w_lo["base"], s, more=True)
                pe.wait_ge(lowt_ready, p + 1)
                nc.tensor.matmul(acc[1 + n][:, :], low_t[:, :], lora_up[:, s], start=False,
                                 stop=True).then_inc(base_acc, 1)

            def attend(moving):
                m = moving.rearrange("p (t c) -> p t c", t=QD)
                for i in range(QD):
                    mm = nc.tensor.matmul(attn_ps[:, i * QD:(i + 1) * QD], diag[:, i, :], m[:, i, :],
                                          start=True, stop=True)
                return mm

            turn_rows(0, xn1_ready, xt_done)

            def step(t, prev, nxt):
                pe.wait_ge(xhi_ready, 2 * t + 2)
                pe.wait_ge(xlo_ready, 2 * t + 2)
                if prev:
                    pe.wait_ge(v_biased, 2 * t)
                project("k", 0, 0, k_acc)
                if prev:
                    pe.wait_ge(base_free, 2 * t - 1)
                project("k", 1, 1, k_acc)
                if prev:
                    turn_rows(t - 1, xn2_ready, x2t_done)
                if prev:
                    pe.wait_ge(base_free, 2 * t)
                project("q", 0, 2, q_acc)
                pe.wait_ge(k_biased, 2 * t + 2)
                if prev:
                    experts(t - 1)
                project("q", 1, 1, q_acc)
                pe.wait_ge(q_biased, 2 * t + 1)
                project("v", 0, 2, v_acc)
                if prev:
                    turn_low(t - 1)
                if nxt:
                    if prev:
                        pe.wait_ge(x2lo_ready, 2 * t)
                    turn_rows(t + 1, xn1_ready, xt_done)
                if prev:
                    pe.wait_ge(low_ready, t)
                project("v", 1, 0, v_acc)
                pe.wait_ge(kt_ready, t + 1)
                pe.wait_ge(qdiag_ready, NQ * (t + 1))
                if prev:
                    pe.wait_ge(ctx_turned, t)
                attend(kt).then_inc(scored, 1)
                if prev:
                    pe.wait_ge(q_biased, 2 * t + 2)
                    dense(t - 1, 0)
                    pe.wait_ge(v_biased, 2 * t + 1)
                    dense(t - 1, 1)
                pe.wait_ge(vdiag_ready, NQ * (t + 1))
                pe.wait_ge(pt_ready, t + 1)
                attend(pt).then_inc(ctx_acc, 1)

            def tail(t):
                turn_rows(t - 1, xn2_ready, x2t_done)
                pe.wait_ge(v_biased, 2 * t)
                experts(t - 1)
                turn_low(t - 1)
                pe.wait_ge(base_free, 2 * t)
                dense(t - 1, 0)
                dense(t - 1, 1)

            pipeline(pe, step, tail)


def kernel(**inputs):
    import numpy as np
    import concourse.bacc as bacc
    from concourse.bass_utils import run_bass_kernel_spmd

    def get(name):
        return np.asarray(inputs[name])

    x = get("L0_attn_hidden_states")
    B, S, D = x.shape
    arrays = {
        "x_dram": x.reshape(B * S, D),
        "wT_dram": np.stack([get("L0_attn_wk").T, get("L0_attn_wq").T, get("L0_attn_wv").T,
                             get("L0_ffn_base_w").T]),
        "agT_dram": np.concatenate([get("L0_ffn_lora_A").reshape(ER, D).T, get("L0_ffn_gate_w").T], axis=1),
        "lora_b_dram": get("L0_ffn_lora_B").transpose(0, 2, 1).reshape(ER, D),
        "bias_dram": np.stack([get("L0_attn_bk"), get("L0_attn_bq"), get("L0_attn_bv"), get("L0_ffn_base_b")]),
    }
    arrays = {n: np.ascontiguousarray(a) for n, a in arrays.items()}
    nc = bacc.Bacc("TRN2", target_bir_lowering=False, num_devices=1, dynamic_dma_scratch_size=1024)
    args = [nc.dram_tensor(n, a.shape, mybir.dt.from_np(a.dtype), kind="ExternalInput").ap()
            for n, a in arrays.items()]
    out = nc.dram_tensor("out_dram", (B * S, D), F32, kind="ExternalOutput").ap()
    block_kernel(nc, *args, out)
    r = run_bass_kernel_spmd(nc, [arrays], core_ids=[0])
    return r.results[0]["out_dram"].reshape(B, S, D)
```

```python
from contextlib import ExitStack

import concourse.bass as bass
from concourse import mybir

P = 128
QD = 32
NQ = P // QD
HID = 1024
HEADS = 32
HD = HID // HEADS
assert HD == QD and HEADS == QD
KC = HID // P
HALF = 512
NB = HID // HALF
EXPERTS = 8
RANK = 16
ER = EXPERTS * RANK
AG = ER + EXPERTS
LORA_SCALING = 32.0 / 16.0
LN_EPS = 1e-5
X_SCALE_EXP = 8
W_SCALE_EXP = 14
SCORE_SCALE = 1.0 / float(HD) ** 0.5

ALU = mybir.AluOpType
ACT = mybir.ActivationFunctionType
AX = mybir.AxisListType
F32 = mybir.dt.float32
F16 = mybir.dt.float16
I32 = mybir.dt.int32
U32 = mybir.dt.uint32
RMAX = bass.bass_isa.ReduceOp.max

GROUPS = ("k", "q", "v", "base")


def block_kernel(nc, x, wT, agT, lora_b, biases, out):
    T = x.shape[0] // P
    with ExitStack() as ctx:
        def sb(name, shape, dt=F32):
            return ctx.enter_context(nc.sbuf_tensor(name, shape, dt))

        def ps(name, shape, dt=F32):
            return ctx.enter_context(nc.psum_tensor(name, shape, dt))

        def sem(name):
            return ctx.enter_context(nc.semaphore(name))

        w_hi = {g: sb(f"w_hi_{g}", [P, KC, HID], F16) for g in GROUPS}
        w_lo = {g: sb(f"w_lo_{g}", [P, KC, HID], F16) for g in GROUPS}
        ag_hi = sb("ag_hi", [P, KC, AG], F16)
        ag_lo = sb("ag_lo", [P, KC, AG], F16)
        lora_up = sb("lora_up", [P, HID])
        bias = {g: sb(f"bias_{g}", [P, HID]) for g in GROUPS}
        ident = sb("ident", [P, P])
        expert_no = sb("expert_no", [P, EXPERTS])
        eps = sb("eps", [P, 1])
        pow_half = sb("pow_half", [P, 1])
        x_scale = sb("x_scale", [P, 1])
        NG = len(GROUPS) + 1
        w_chunk_sum = sb("w_chunk_sum", [P, NG, KC])
        w_part_max = sb("w_part_max", [P, NG])
        w_max = sb("w_max", [P, NG])
        w_clamped = sb("w_clamped", [P, NG])
        w_exp = sb("w_exp", [P, NG], I32)
        w_scale_bits = sb("w_scale_bits", [P, NG], I32)
        w_undo_bits = sb("w_undo_bits", [P, NG], I32)
        w_scale = w_scale_bits[:, :].bitcast(F32)
        w_undo = w_undo_bits[:, :].bitcast(F32)
        lora_scale0 = sb("lora_scale0", [P, 1])
        lora_scale = sb("lora_scale", [P, 1])

        block_diag_len = QD * P
        work = sb("work", [P, block_diag_len + 9 * HID])
        at = [0]

        def carve(n):
            at[0] += n
            return work[:, at[0] - n:at[0]]

        stage = work[:, 0:KC * HID].rearrange("p (k n) -> p k n", k=KC)
        ag_stage = work[:, 0:KC * AG].rearrange("p (k n) -> p k n", k=KC)
        AG_CHUNKS = -(-KC * AG // HID)
        diag = carve(block_diag_len).rearrange("p (t c) -> p t c", t=QD)
        res = carve(HID)
        x1 = carve(HID)
        soft = carve(HID)
        pt = carve(HID)
        assert at[0] == KC * HID
        ld = carve(HID)
        xn = carve(HID)
        ev = carve(HID)
        kt = carve(HID)
        turned = carve(HID)
        y = kt
        lo_top = sb("lo_top", [P, 3])
        lo_top_all = sb("lo_top_all", [P, 1])
        lo_flag = sb("lo_flag", [P, 1])
        lo_flag_all = sb("lo_flag_all", [P, 1])
        lo_flag_int = sb("lo_flag_int", [P, 1], I32)
        turned3 = turned.rearrange("p (t c) -> p t c", t=QD)
        x_hi = sb("x_hi", [P, KC, P], F16)
        x_lo = sb("x_lo", [P, KC, P], F16)
        x2_hi = sb("x2_hi", [P, KC, P], F16)
        x2_lo = sb("x2_lo", [P, KC, P], F16)
        low = sb("low", [P, ER])
        low_t = sb("low_t", [P, P])
        stats = sb("stats", [P, 2, 2, 6])
        mv = sb("mv", [P, 2, 2])
        var = sb("var", [P, 2])
        root_var = sb("root_var", [P, 2])
        rstd = sb("rstd", [P, 2])
        top = sb("top", [P, QD])
        den = sb("den", [P, QD])
        inv = sb("inv", [P, QD])
        logits = sb("logits", [P, EXPERTS])
        best = sb("best", [P, 8])
        best_at = sb("best_at", [P, 8], U32)
        best_no = sb("best_no", [P, 8])
        gap = sb("gap", [P, 1])
        e2 = sb("e2", [P, 1])
        e_sum = sb("e_sum", [P, 1])
        w1 = sb("w1", [P, 1])
        w2 = sb("w2", [P, 1])
        hot1 = sb("hot1", [P, EXPERTS])
        hot2 = sb("hot2", [P, EXPERTS])
        w_full = sb("w_full", [P, EXPERTS])

        acc = [ps(f"acc{i}", [P, HALF]) for i in range(3)]
        turn_ps = ps("turn_ps", [P, HID])
        attn_ps = ps("attn_ps", [P, HID])
        low_ps = ps("low_ps", [P, HALF])

        w_loaded = [sem(f"w_loaded{k}") for k in range(KC)]
        ag_loaded = sem("ag_loaded")
        const_loaded = sem("const_loaded")
        ident_zero = sem("ident_zero")
        consts_set = sem("consts_set")
        sum_chunk = sem("sum_chunk")
        max_part = sem("max_part")
        max_all = sem("max_all")
        scale_step = sem("scale_step")
        scale_ready = sem("scale_ready")
        undo_ready = sem("undo_ready")
        w_hi_act = sem("w_hi_act")
        w_hi_dve = sem("w_hi_dve")
        lo_step = sem("lo_step")
        lo_flagged = sem("lo_flagged")
        lo_reduced = sem("lo_reduced")
        flag_ready = sem("flag_ready")
        w_lo_done = sem("w_lo_done")
        diag_zero = sem("diag_zero")
        lora_scaled = sem("lora_scaled")

        ld_loaded = sem("ld_loaded")
        res_loaded = sem("res_loaded")
        y_stored = sem("y_stored")
        mv1 = sem("mv1")
        var1 = sem("var1")
        root1 = sem("root1")
        rstd1 = sem("rstd1")
        xn1_ready = sem("xn1_ready")
        xt_done = sem("xt_done")
        xhi_ready = sem("xhi_ready")
        xlo_ready = sem("xlo_ready")
        k_acc = sem("k_acc")
        q_acc = sem("q_acc")
        v_acc = sem("v_acc")
        k_biased = sem("k_biased")
        q_biased = sem("q_biased")
        v_biased = sem("v_biased")
        kt_ready = sem("kt_ready")
        qt_ready = sem("qt_ready")
        vt_ready = sem("vt_ready")
        qdiag_ready = sem("qdiag_ready")
        vdiag_ready = sem("vdiag_ready")
        scored = sem("scored")
        top_ready = sem("top_ready")
        shifted = sem("shifted")
        exped = sem("exped")
        den_ready = sem("den_ready")
        inv_ready = sem("inv_ready")
        prob_ready = sem("prob_ready")
        pt_ready = sem("pt_ready")
        ctx_acc = sem("ctx_acc")
        ctx_turned = sem("ctx_turned")
        x1_ready = sem("x1_ready")
        mv2 = sem("mv2")
        var2 = sem("var2")
        root2 = sem("root2")
        rstd2 = sem("rstd2")
        xn2_ready = sem("xn2_ready")
        x1_biased = sem("x1_biased")
        x2t_done = sem("x2t_done")
        x2hi_ready = sem("x2hi_ready")
        x2lo_ready = sem("x2lo_ready")
        ag_acc = sem("ag_acc")
        best_ready = sem("best_ready")
        best_found = sem("best_found")
        gap_ready = sem("gap_ready")
        e2_ready = sem("e2_ready")
        no_ready = sem("no_ready")
        e_summed = sem("e_summed")
        w1_ready = sem("w1_ready")
        w2_ready = sem("w2_ready")
        hots_ready = sem("hots_ready")
        full_ready = sem("full_ready")
        low_ready = sem("low_ready")
        low_turned = sem("low_turned")
        lowt_ready = sem("lowt_ready")
        base_acc = sem("base_acc")
        base_free = sem("base_free")

        block = ctx.enter_context(nc.Block())
        ACT_HI = 5
        n_split = NG * KC

        def rows(ap, t):
            return ap[bass.ds(t * P, P), :]

        def pipeline(eng, step, tail):
            step(0, prev=False, nxt=True)
            with eng.Fori(1, T - 1) as t:
                step(t, prev=True, nxt=True)
            step(T - 1, prev=True, nxt=False)
            tail(T)

        @block.sync
        def _(sp):
            sp.dma_start(ld, rows(x, 0)).then_inc(ld_loaded, 16)
            for j in range(len(GROUPS)):
                for k in range(KC):
                    if j:
                        sp.wait_ge(w_lo_done, (j - 1) * KC + k + 1)
                    sp.dma_start(stage[:, k, :], wT[j, k * P:(k + 1) * P, :]).then_inc(w_loaded[k], 16)
                if j == 0:
                    for b, g in enumerate(GROUPS):
                        sp.dma_start(bias[g][:, :], biases[b:b + 1, :].to_broadcast([P, HID])).then_inc(
                            const_loaded, 16)
                    sp.dma_start(lora_up[:, :], lora_b).then_inc(const_loaded, 16)
                    sp.wait_ge(xn1_ready, 1)
                    sp.dma_start(ld, rows(x, 1)).then_inc(ld_loaded, 16)
            sp.wait_ge(w_lo_done, (len(GROUPS) - 1) * KC + AG_CHUNKS)
            sp.dma_start(ag_stage, agT.rearrange("(k p) n -> p k n", p=P)).then_inc(ag_loaded, 16)
            sp.wait_ge(w_lo_done, n_split)
            sp.dma_start(res, rows(x, 0)).then_inc(res_loaded, 16)

            def store(p):
                sp.wait_ge(base_free, 2 * p + 4)
                sp.dma_start(rows(out, p), y).then_inc(y_stored, 16)

            def step(t, prev, nxt):
                if prev and nxt:
                    sp.wait_ge(xn1_ready, t + 1)
                    sp.dma_start(ld, rows(x, t + 1)).then_inc(ld_loaded, 16)
                if prev:
                    sp.wait_ge(x1_ready, t)
                    sp.dma_start(res, rows(x, t)).then_inc(res_loaded, 16)
                    store(t - 1)

            pipeline(sp, step, lambda t: store(t - 1))
            sp.wait_ge(y_stored, 16 * (T + 1))

        @block.gpsimd
        def _(pool):
            def root(t, i, mv_ready, var_ready, root_ready, rstd_ready):
                pool.wait_ge(mv_ready, t + 1)
                nc.gpsimd.tensor_tensor(var[:, i:i + 1], mv[:, i, 1:2], eps[:, :], ALU.add).then_inc(var_ready, 1)
                pool.wait_ge(var_ready, t + 1)
                nc.gpsimd.tensor_tensor(root_var[:, i:i + 1], var[:, i:i + 1], pow_half[:, :],
                                        ALU.pow).then_inc(root_ready, 1)
                pool.wait_ge(root_ready, t + 1)
                nc.gpsimd.tensor_tensor(rstd[:, i:i + 1], root_var[:, i:i + 1], x_scale[:, :],
                                        ALU.mult).then_inc(rstd_ready, 1)

            nc.gpsimd.memset(ident[:, :], 0.0).then_inc(ident_zero, 1)
            pool.wait_ge(ident_zero, 1)
            nc.gpsimd.affine_select(out=ident[:, :], in_=ident[:, :], compare_op=ALU.not_equal, fill=1.0, base=0,
                                    pattern=[[-1, P]], channel_multiplier=1).then_inc(consts_set, 1)
            for e in range(EXPERTS):
                nc.gpsimd.memset(expert_no[:, e:e + 1], float(e)).then_inc(consts_set, 1)
            nc.gpsimd.memset(eps[:, :], LN_EPS).then_inc(consts_set, 1)
            nc.gpsimd.memset(pow_half[:, :], -0.5).then_inc(consts_set, 1)
            nc.gpsimd.memset(x_scale[:, :], 2.0 ** X_SCALE_EXP).then_inc(consts_set, 1)
            pool.wait_ge(consts_set, EXPERTS + 4)
            root(0, 0, mv1, var1, root1, rstd1)
            for j in range(NG):
                pool.wait_ge(max_part, j + 1)
                nc.gpsimd.partition_all_reduce(w_max[:, j:j + 1], w_part_max[:, j:j + 1], P, RMAX).then_inc(max_all, 1)


            pool.wait_ge(w_lo_done, n_split)
            nc.gpsimd.memset(diag, 0.0).then_inc(diag_zero, 1)
            pool.wait_ge(const_loaded, 16 * (len(GROUPS) + 1))

            def norm2(p):
                root(p, 1, mv2, var2, root2, rstd2)

            def base_bias(p):
                pool.wait_ge(xn2_ready, p + 1)
                nc.gpsimd.tensor_tensor(x1, x1, bias["base"][:, :], ALU.add).then_inc(x1_biased, 1)

            def spread(ready):
                for g in (2, 3):
                    s = slice(g * QD, (g + 1) * QD)
                    nc.gpsimd.tensor_copy(diag[s, :, s], turned3[s, :, :]).then_inc(ready, 1)
                    pool.drain()

            def step(t, prev, nxt):
                if nxt:
                    pool.wait_ge(xn1_ready, t + 1)
                    root(t + 1, 0, mv1, var1, root1, rstd1)
                if prev:
                    norm2(t - 1)
                pool.drain()
                pool.wait_ge(diag_zero, 1)
                pool.wait_ge(qt_ready, t + 1)
                if prev:
                    pool.wait_ge(ctx_acc, t)
                spread(qdiag_ready)
                if prev:
                    base_bias(t - 1)
                else:
                    pool.wait_ge(lo_flagged, 1)
                    nc.gpsimd.partition_all_reduce(lo_flag_all[:, :], lo_flag[:, :], P, RMAX).then_inc(lo_reduced, 1)
                pool.drain()
                pool.wait_ge(diag_zero, 1)
                pool.wait_ge(vt_ready, t + 1)
                pool.wait_ge(scored, t + 1)
                spread(vdiag_ready)

            def tail(t):
                norm2(t - 1)
                base_bias(t - 1)

            pipeline(pool, step, tail)

        @block.scalar
        def _(act):
            def prepare(j, staged, hi, loaded, count):
                for k in range(KC):
                    act.wait_ge(loaded[k], count)
                    nc.scalar.activation(hi[:, k, :], staged[:, k, :], ACT.Abs,
                                         accum_out=w_chunk_sum[:, j, k:k + 1]).then_inc(sum_chunk, 1)
                act.wait_ge(scale_ready, j + 1)
                for k in range(ACT_HI):
                    nc.scalar.activation(hi[:, k, :], staged[:, k, :], ACT.Copy,
                                         scale=w_scale[:, j:j + 1]).then_inc(w_hi_act, 1)

            def rows_hi(t, dst, done, ready):
                for h in range(2):
                    act.wait_ge(done, 2 * t + h + 1)
                    c = KC // 2
                    nc.scalar.copy(dst[:, h * c:(h + 1) * c, :],
                                   turn_ps[:, h * HALF:(h + 1) * HALF].rearrange("p (k n) -> p k n", k=c)
                                   ).then_inc(ready, 1)

            def spread(ready):
                for g in (0, 1):
                    s = slice(g * QD, (g + 1) * QD)
                    nc.scalar.copy(diag[s, :, s], turned3[s, :, :]).then_inc(ready, 1)

            rows_hi(0, x_hi, xt_done, xhi_ready)
            for j, g in enumerate(GROUPS):
                prepare(j, stage, w_hi[g], w_loaded, 16 * (j + 1))
            prepare(NG - 1, ag_stage, ag_hi, [ag_loaded] * KC, 16)
            act.wait_ge(diag_zero, 1)

            def gate_exp(p):
                act.wait_ge(gap_ready, p + 1)
                nc.scalar.activation(e2[:, :], gap[:, :], ACT.Exp).then_inc(e2_ready, 1)

            def low_copy(p):
                act.wait_ge(low_turned, p + 1)
                nc.scalar.copy(low_t[:, :], low_ps[:, 0:P]).then_inc(lowt_ready, 1)

            def step(t, prev, nxt):
                act.wait_ge(qt_ready, t + 1)
                if prev:
                    act.wait_ge(ctx_acc, t)
                spread(qdiag_ready)
                if prev:
                    rows_hi(t - 1, x2_hi, x2t_done, x2hi_ready)
                    gate_exp(t - 1)
                if nxt:
                    act.wait_ge(v_acc, 2 * t + 2)
                    rows_hi(t + 1, x_hi, xt_done, xhi_ready)
                if prev:
                    low_copy(t - 1)
                act.wait_ge(shifted, t + 1)
                nc.scalar.activation(soft, soft, ACT.Exp, scale=SCORE_SCALE).then_inc(exped, 1)
                act.wait_ge(vt_ready, t + 1)
                act.wait_ge(scored, t + 1)
                spread(vdiag_ready)

            def tail(t):
                rows_hi(t - 1, x2_hi, x2t_done, x2hi_ready)
                gate_exp(t - 1)
                low_copy(t - 1)

            pipeline(act, step, tail)

        @block.vector
        def _(dve):
            nc.vector.memset(low[:, :], 0.0).then_inc(base_free, 2)
            nc.vector.memset(logits[:, :], 0.0).then_inc(y_stored, 16)

            def prepare(j, staged, hi, lo):
                dve.wait_ge(sum_chunk, KC * (j + 1))
                nc.vector.tensor_reduce(w_part_max[:, j:j + 1], w_chunk_sum[:, j, :], AX.X,
                                        ALU.max).then_inc(max_part, 1)
                if 1 <= j <= 3:
                    nc.vector.tensor_reduce(lo_top[:, j - 1:j],
                                            w_lo[GROUPS[j - 1]][:, :, :].rearrange("p k n -> p (k n)"), AX.X,
                                            ALU.max, apply_absolute_value=True).then_inc(lo_step, 1)
                dve.wait_ge(max_all, j + 1)
                nc.vector.tensor_scalar(w_clamped[:, j:j + 1], w_max[:, j:j + 1], 2.0 ** -90, None,
                                        ALU.max).then_inc(scale_step, 1)
                dve.wait_ge(scale_step, 2 * j + 1)
                nc.vector.tensor_single_scalar(w_exp[:, j:j + 1], w_clamped[:, j:j + 1].bitcast(I32), 0x7F800000,
                                               ALU.bitwise_and).then_inc(scale_step, 1)
                dve.wait_ge(scale_step, 2 * j + 2)
                nc.vector.tensor_scalar(w_scale_bits[:, j:j + 1], w_exp[:, j:j + 1], -1.0,
                                        float((W_SCALE_EXP + 254) << 23), ALU.mult, ALU.add).then_inc(scale_ready, 1)
                nc.vector.tensor_scalar(w_undo_bits[:, j:j + 1], w_exp[:, j:j + 1],
                                        float((W_SCALE_EXP + X_SCALE_EXP) << 23), None, ALU.subtract
                                        ).then_inc(undo_ready, 1)
                dve.wait_ge(scale_ready, j + 1)
                for k in range(ACT_HI, KC):
                    nc.vector.tensor_scalar(hi[:, k, :], staged[:, k, :], w_scale[:, j:j + 1], None,
                                            ALU.mult).then_inc(w_hi_dve, 1)
                for k in range(KC):
                    if k < ACT_HI:
                        dve.wait_ge(w_hi_act, j * ACT_HI + k + 1)
                    else:
                        dve.wait_ge(w_hi_dve, j * (KC - ACT_HI) + k - ACT_HI + 1)
                    nc.vector.scalar_tensor_tensor(out=lo[:, k, :], in0=staged[:, k, :],
                                                   scalar=w_scale[:, j:j + 1], in1=hi[:, k, :], op0=ALU.mult,
                                                   op1=ALU.subtract).then_inc(w_lo_done, 1)

            def prepare_group(g):
                j = GROUPS.index(g)
                prepare(j, stage, w_hi[g], w_lo[g])

            def prepare_experts():
                prepare(NG - 1, ag_stage, ag_hi, ag_lo)
                dve.wait_ge(undo_ready, NG)
                nc.vector.tensor_tensor(lora_scale0[:, :], w_undo[:, NG - 1:NG], w_scale[:, NG - 2:NG - 1],
                                        ALU.mult).then_inc(lora_scaled, 1)
                dve.wait_ge(lora_scaled, 1)
                nc.vector.tensor_scalar(lora_scale[:, :], lora_scale0[:, :], 2.0 ** X_SCALE_EXP * LORA_SCALING,
                                        None, ALU.mult).then_inc(lora_scaled, 1)
                dve.wait_ge(lora_scaled, 2)

            def flag_low_parts():
                dve.wait_ge(lo_step, 3)
                nc.vector.tensor_reduce(lo_top_all[:, :], lo_top[:, :], AX.X, ALU.max).then_inc(lo_step, 1)
                dve.wait_ge(lo_step, 4)
                nc.vector.tensor_scalar(lo_flag[:, :], lo_top_all[:, :], 0.0, None, ALU.not_equal).then_inc(lo_flagged, 1)

            def publish_flag():
                dve.wait_ge(lo_reduced, 1)
                nc.vector.tensor_copy(lo_flag_int[:, :], lo_flag_all[:, :]).then_inc(flag_ready, 1)

            def ln_stats(i, src, mean_ready):
                for h in range(2):
                    nc.vector.bn_stats(stats[:, i, h, :], src[:, h * HALF:(h + 1) * HALF])
                dve.drain()
                nc.vector.bn_aggr(mv[:, i, :], stats[:, i, :, :].rearrange("p a b -> p (a b)")).then_inc(mean_ready, 1)

            def normalise(t, i, src, rstd_ready, ready):
                dve.wait_ge(rstd_ready, t + 1)
                nc.vector.tensor_scalar(xn, src, mv[:, i, 0:1], rstd[:, i:i + 1], ALU.subtract,
                                        ALU.mult).then_inc(ready, 1)

            def rows_lo(t, dst, hi, hi_ready, ready):
                c = KC // 2
                for h in range(2):
                    dve.wait_ge(hi_ready, 2 * t + h + 1)
                    nc.vector.tensor_tensor(dst[:, h * c:(h + 1) * c, :],
                                            turn_ps[:, h * HALF:(h + 1) * HALF].rearrange("p (k n) -> p k n", k=c),
                                            hi[:, h * c:(h + 1) * c, :], ALU.subtract).then_inc(ready, 1)

            def add_bias(t, n, g, j, bank, acc_done, biased):
                dve.wait_ge(acc_done, 2 * t + n + 1)
                s = slice(n * HALF, (n + 1) * HALF)
                nc.vector.scalar_tensor_tensor(out=ev[:, s], in0=acc[bank][:, :], scalar=w_undo[:, j:j + 1],
                                               in1=bias[g][:, s], op0=ALU.mult, op1=ALU.add).then_inc(biased, 1)

            ev_heads = ev.rearrange("p (h d) -> p h d", h=HEADS)

            dve.wait_ge(ld_loaded, 16)
            ln_stats(0, ld, mv1)
            normalise(0, 0, ld, rstd1, xn1_ready)
            rows_lo(0, x_lo, x_hi, xhi_ready, xlo_ready)
            prepare_group("k")
            prepare_group("q")
            dve.wait_ge(const_loaded, 16 * (len(GROUPS) + 1))
            dve.wait_ge(consts_set, EXPERTS + 4)

            def gating(p):
                dve.wait_ge(ag_acc, p + 1)
                nc.vector.tensor_scalar(logits[:, :], acc[0][:, ER:AG], w_undo[:, NG - 1:NG], None,
                                        ALU.mult)
                dve.drain()
                nc.vector.max(best[:, :], logits[:, :]).then_inc(best_ready, 1)
                dve.wait_ge(best_ready, p + 1)
                nc.vector.tensor_tensor(gap[:, :], best[:, 1:2], best[:, 0:1], ALU.subtract).then_inc(gap_ready, 1)
                nc.vector.max_index(best_at[:, :], best[:, :], logits[:, :]).then_inc(best_found, 1)
                dve.wait_ge(best_found, p + 1)
                nc.vector.tensor_copy(best_no[:, :], best_at[:, :]).then_inc(no_ready, 1)
                dve.wait_ge(e2_ready, p + 1)
                nc.vector.tensor_scalar(e_sum[:, :], e2[:, :], 1.0, None, ALU.add).then_inc(e_summed, 1)
                dve.wait_ge(e_summed, p + 1)
                nc.vector.reciprocal(w1[:, :], e_sum[:, :]).then_inc(w1_ready, 1)
                dve.wait_ge(w1_ready, p + 1)
                nc.vector.tensor_tensor(w2[:, :], e2[:, :], w1[:, :], ALU.mult).then_inc(w2_ready, 1)
                dve.wait_ge(no_ready, p + 1)
                nc.vector.tensor_scalar(hot1[:, :], expert_no[:, :], best_no[:, 0:1], w1[:, 0:1], ALU.is_equal,
                                        ALU.mult).then_inc(hots_ready, 1)
                dve.wait_ge(w2_ready, p + 1)
                nc.vector.tensor_scalar(hot2[:, :], expert_no[:, :], best_no[:, 1:2], w2[:, 0:1], ALU.is_equal,
                                        ALU.mult).then_inc(hots_ready, 1)
                dve.wait_ge(hots_ready, 2 * p + 2)
                nc.vector.tensor_tensor(w_full[:, :], hot1[:, :], hot2[:, :], ALU.add).then_inc(full_ready, 1)
                dve.wait_ge(full_ready, p + 1)
                nc.vector.scalar_tensor_tensor(
                    out=low[:, :].rearrange("p (e r) -> p e r", e=EXPERTS),
                    in0=acc[0][:, 0:ER].rearrange("p (e r) -> p e r", e=EXPERTS), scalar=lora_scale[:, 0:1],
                    in1=w_full[:, :].unsqueeze(2).to_broadcast([P, EXPERTS, RANK]),
                    op0=ALU.mult, op1=ALU.mult).then_inc(low_ready, 1)

            def finish(p, n):
                s = slice(n * HALF, (n + 1) * HALF)
                if n == 0:
                    dve.wait_ge(x1_biased, p + 1)
                dve.wait_ge(base_acc, 2 * p + n + 1)
                nc.vector.scalar_tensor_tensor(out=y[:, s], in0=acc[1 + n][:, :], scalar=w_undo[:, NG - 2:NG - 1],
                                               in1=x1[:, s], op0=ALU.mult, op1=ALU.add).then_inc(base_free, 1)

            def attention_end(p):
                dve.wait_ge(ctx_acc, p + 1)
                nc.vector.transpose(ev_heads, attn_ps[:, :].rearrange("p (t h) -> p h t", t=QD)
                                    ).then_inc(ctx_turned, 1)
                dve.wait_ge(ctx_turned, p + 1)
                dve.wait_ge(res_loaded, 16 * (p + 1))
                dve.wait_ge(base_free, 2 * p + 2)
                nc.vector.tensor_tensor(x1, ev, res, ALU.add).then_inc(x1_ready, 1)
                dve.wait_ge(x1_ready, p + 1)

            def norm2(p):
                dve.wait_ge(xt_done, 2 * p + 2)
                normalise(p, 1, x1, rstd2, xn2_ready)

            def step(t, prev, nxt):
                add_bias(t, 0, "k", 0, 0, k_acc, k_biased)
                if nxt:
                    dve.wait_ge(ld_loaded, 16 * (t + 2))
                    ln_stats(0, ld, mv1)
                add_bias(t, 1, "k", 0, 1, k_acc, k_biased)
                dve.wait_ge(k_biased, 2 * t + 2)
                if prev:
                    dve.wait_ge(y_stored, 16 * t)
                nc.vector.transpose(kt.rearrange("p (t h) -> p h t", t=QD), ev_heads).then_inc(kt_ready, 1)
                dve.wait_ge(kt_ready, t + 1)
                if prev:
                    attention_end(t - 1)
                else:
                    prepare_group("v")
                add_bias(t, 0, "q", 1, 2, q_acc, q_biased)
                if prev:
                    ln_stats(1, x1, mv2)
                add_bias(t, 1, "q", 1, 0, q_acc, q_biased)
                dve.wait_ge(q_biased, 2 * t + 2)
                if prev:
                    dve.wait_ge(vdiag_ready, NQ * t)
                nc.vector.transpose(turned.rearrange("p (t h) -> p h t", t=QD), ev_heads).then_inc(qt_ready, 1)
                if prev:
                    norm2(t - 1)
                else:
                    prepare_group("base")
                    prepare_experts()
                dve.wait_ge(qt_ready, t + 1)
                add_bias(t, 0, "v", 2, 1, v_acc, v_biased)
                if prev:
                    rows_lo(t - 1, x2_lo, x2_hi, x2hi_ready, x2lo_ready)
                if nxt:
                    if prev:
                        dve.wait_ge(x2t_done, 2 * t)
                    normalise(t + 1, 0, ld, rstd1, xn1_ready)
                add_bias(t, 1, "v", 2, 2, v_acc, v_biased)
                dve.wait_ge(v_biased, 2 * t + 2)
                dve.wait_ge(qdiag_ready, NQ * (t + 1))
                nc.vector.transpose(turned.rearrange("p (t d) -> p d t", t=QD),
                                    ev.rearrange("p (h d) -> p d h", h=HEADS)).then_inc(vt_ready, 1)
                dve.wait_ge(vt_ready, t + 1)
                if prev:
                    gating(t - 1)
                if nxt:
                    dve.wait_ge(v_acc, 2 * t + 2)
                    rows_lo(t + 1, x_lo, x_hi, xhi_ready, xlo_ready)
                if not prev:
                    flag_low_parts()
                dve.wait_ge(scored, t + 1)
                scores = attn_ps[:, :].rearrange("p (t c) -> p t c", t=QD)
                s3 = soft.rearrange("p (t c) -> p t c", t=QD)
                nc.vector.tensor_reduce(top[:, :], scores, AX.X, ALU.max).then_inc(top_ready, 1)
                dve.wait_ge(top_ready, t + 1)
                nc.vector.tensor_tensor(s3, scores, top[:, :].unsqueeze(2).to_broadcast([P, QD, QD]),
                                        ALU.subtract).then_inc(shifted, 1)
                if prev:
                    finish(t - 1, 0)
                dve.wait_ge(exped, t + 1)
                nc.vector.tensor_reduce(den[:, :], s3, AX.X, ALU.add).then_inc(den_ready, 1)
                dve.wait_ge(den_ready, t + 1)
                nc.vector.reciprocal(inv[:, :], den[:, :]).then_inc(inv_ready, 1)
                dve.wait_ge(inv_ready, t + 1)
                nc.vector.tensor_tensor(s3, s3, inv[:, :].unsqueeze(2).to_broadcast([P, QD, QD]),
                                        ALU.mult).then_inc(prob_ready, 1)
                dve.wait_ge(prob_ready, t + 1)
                if prev:
                    dve.wait_ge(ctx_acc, t)
                nc.vector.transpose(pt, soft).then_inc(pt_ready, 1)
                if prev:
                    finish(t - 1, 1)
                else:
                    publish_flag()
                dve.wait_ge(pt_ready, t + 1)

            def tail(t):
                attention_end(t - 1)
                ln_stats(1, x1, mv2)
                norm2(t - 1)
                rows_lo(t - 1, x2_lo, x2_hi, x2hi_ready, x2lo_ready)
                gating(t - 1)
                dve.wait_ge(y_stored, 16 * t)
                finish(t - 1, 0)
                finish(t - 1, 1)

            pipeline(dve, step, tail)

        @block.tensor
        def _(pe):
            pe.wait_ge(consts_set, EXPERTS + 4)

            def turn_rows(t, xn_ready, done):
                pe.wait_ge(xn_ready, t + 1)
                for k in range(KC):
                    mm = nc.tensor.transpose(turn_ps[:, k * P:(k + 1) * P], xn[:, k * P:(k + 1) * P], ident[:, :])
                    if k % (KC // 2) == KC // 2 - 1:
                        mm.then_inc(done, 1)

            def attend_one(moving, i):
                return nc.tensor.matmul(attn_ps[:, i * QD:(i + 1) * QD], diag[:, i, :],
                                        moving[:, i * QD:(i + 1) * QD], start=True, stop=True)

            def project(t, g, n, bank, done, any_low, moving=None, first=0, attended=None):
                cols = slice(n * HALF, (n + 1) * HALF)
                dst = acc[bank][:, :]
                for k in range(KC):
                    nc.tensor.matmul(dst, x_hi[:, k, :], w_hi[g][:, k, cols], start=(k == 0), stop=False)
                    if moving is not None:
                        attend_one(moving, first + k)
                if any_low is None:
                    for k in range(KC):
                        nc.tensor.matmul(dst, x_hi[:, k, :], w_lo[g][:, k, cols], start=False, stop=False)
                else:
                    with pe.If(any_low > 0):
                        for k in range(KC):
                            nc.tensor.matmul(dst, x_hi[:, k, :], w_lo[g][:, k, cols], start=False, stop=False)
                for k in range(KC):
                    mm = nc.tensor.matmul(dst, x_lo[:, k, :], w_hi[g][:, k, cols], start=False, stop=(k == KC - 1))
                    if k == KC - 1:
                        mm.then_inc(done, 1)
                    if moving is not None:
                        small = attend_one(moving, first + KC + k)
                if attended is not None:
                    small.then_inc(attended, 1)

            def experts(p):
                pe.wait_ge(x2hi_ready, 2 * p + 2)
                pe.wait_ge(x2lo_ready, 2 * p + 2)
                dst = acc[0][:, 0:AG]
                for k in range(KC):
                    nc.tensor.matmul(dst, x2_hi[:, k, :], ag_hi[:, k, :], start=(k == 0), stop=False)
                    nc.tensor.matmul(dst, x2_hi[:, k, :], ag_lo[:, k, :], start=False, stop=False)
                    mm = nc.tensor.matmul(dst, x2_lo[:, k, :], ag_hi[:, k, :], start=False, stop=(k == KC - 1))
                mm.then_inc(ag_acc, 1)

            def turn_low(p):
                pe.wait_ge(low_ready, p + 1)
                nc.tensor.transpose(low_ps[:, 0:P], low[:, :], ident[:, :]).then_inc(low_turned, 1)

            def dense(n, moving=None, tokens=range(0)):
                cols = slice(n * HALF, (n + 1) * HALF)
                dst = acc[1 + n][:, :]
                parts = ((x2_hi, w_hi["base"]), (x2_hi, w_lo["base"]), (x2_lo, w_hi["base"]))
                for m in range(3 * KC):
                    rows_part, w_part = parts[m % 3]
                    nc.tensor.matmul(dst, rows_part[:, m // 3, :], w_part[:, m // 3, cols], start=(m == 0),
                                     stop=False)
                    if m < len(tokens):
                        small = attend_one(moving, tokens[m])
                        if tokens[m] == QD - 1:
                            small.then_inc(scored, 1)

            def dense_lora(p):
                pe.wait_ge(lowt_ready, p + 1)
                for n in range(NB):
                    nc.tensor.matmul(acc[1 + n][:, :], low_t[:, :], lora_up[:, n * HALF:(n + 1) * HALF],
                                     start=False, stop=True).then_inc(base_acc, 1)

            def context_ready(p):
                pe.wait_ge(vdiag_ready, NQ * (p + 1))
                pe.wait_ge(pt_ready, p + 1)

            turn_rows(0, xn1_ready, xt_done)
            any_low = [None]

            def step(t, prev, nxt):
                pe.wait_ge(xhi_ready, 2 * t + 2)
                pe.wait_ge(xlo_ready, 2 * t + 2)
                if not prev:
                    pe.wait_ge(w_lo_done, KC)
                else:
                    pe.wait_ge(q_biased, 2 * t)
                project(t, "k", 0, 0, k_acc, any_low[0])
                if prev:
                    pe.wait_ge(base_free, 2 * t - 1)
                    context_ready(t - 1)
                project(t, "k", 1, 1, k_acc, any_low[0], moving=pt if prev else None)
                if prev:
                    pe.wait_ge(base_free, 2 * t)
                else:
                    pe.wait_ge(w_lo_done, 2 * KC)
                project(t, "q", 0, 2, q_acc, any_low[0], moving=pt if prev else None, first=2 * KC,
                        attended=ctx_acc if prev else None)
                pe.wait_ge(k_biased, 2 * t + 2)
                project(t, "q", 1, 0, q_acc, any_low[0])
                if not prev:
                    pe.wait_ge(w_lo_done, 3 * KC)
                project(t, "v", 0, 1, v_acc, any_low[0])
                if prev:
                    turn_rows(t - 1, xn2_ready, x2t_done)
                pe.wait_ge(q_biased, 2 * t + 1)
                project(t, "v", 1, 2, v_acc, any_low[0])
                if prev:
                    pe.wait_ge(q_biased, 2 * t + 2)
                    experts(t - 1)
                if nxt:
                    if prev:
                        pe.wait_ge(x2lo_ready, 2 * t)
                    turn_rows(t + 1, xn1_ready, xt_done)
                pe.wait_ge(kt_ready, t + 1)
                pe.wait_ge(qdiag_ready, NQ * (t + 1))
                if prev:
                    pe.wait_ge(ctx_turned, t)
                    pe.wait_ge(v_biased, 2 * t + 1)
                    dense(0, kt, range(3 * KC))
                    turn_low(t - 1)
                    pe.wait_ge(v_biased, 2 * t + 2)
                    dense(1, kt, range(3 * KC, QD))
                    dense_lora(t - 1)
                else:
                    for i in range(QD):
                        small = attend_one(kt, i)
                    small.then_inc(scored, 1)
                    pe.wait_ge(flag_ready, 1)
                    any_low[0] = pe.value_load(lo_flag_int[0:1, 0:1], min_val=0, max_val=1)

            def tail(t):
                context_ready(t - 1)
                for i in range(QD):
                    small = attend_one(pt, i)
                small.then_inc(ctx_acc, 1)
                turn_rows(t - 1, xn2_ready, x2t_done)
                pe.wait_ge(low_ready, t - 1)
                experts(t - 1)
                pe.wait_ge(base_free, 2 * t)
                dense(0)
                turn_low(t - 1)
                dense(1)
                dense_lora(t - 1)

            pipeline(pe, step, tail)


def kernel(**inputs):
    import numpy as np
    import concourse.bacc as bacc
    from concourse.bass_utils import run_bass_kernel_spmd

    def get(name):
        return np.asarray(inputs[name])

    x = get("L0_attn_hidden_states")
    B, S, D = x.shape
    arrays = {
        "x_dram": x.reshape(B * S, D),
        "wT_dram": np.stack([get("L0_attn_wk").T, get("L0_attn_wq").T, get("L0_attn_wv").T,
                             get("L0_ffn_base_w").T]),
        "agT_dram": np.concatenate([get("L0_ffn_lora_A").reshape(ER, D).T, get("L0_ffn_gate_w").T], axis=1),
        "lora_b_dram": get("L0_ffn_lora_B").transpose(0, 2, 1).reshape(ER, D),
        "bias_dram": np.stack([get("L0_attn_bk"), get("L0_attn_bq"), get("L0_attn_bv"), get("L0_ffn_base_b")]),
    }
    arrays = {n: np.ascontiguousarray(a) for n, a in arrays.items()}
    nc = bacc.Bacc("TRN2", target_bir_lowering=False, num_devices=1, dynamic_dma_scratch_size=1024)
    args = [nc.dram_tensor(n, a.shape, mybir.dt.from_np(a.dtype), kind="ExternalInput").ap()
            for n, a in arrays.items()]
    out = nc.dram_tensor("out_dram", (B * S, D), F32, kind="ExternalOutput").ap()
    block_kernel(nc, *args, out)
    r = run_bass_kernel_spmd(nc, [arrays], core_ids=[0])
    return r.results[0]["out_dram"].reshape(B, S, D)
```

```python
from contextlib import ExitStack

import concourse.bass as bass
from concourse import mybir

P = 128
QD = 32
NQ = P // QD
HID = 1024
HEADS = 32
HD = HID // HEADS
assert HD == QD and HEADS == QD
KC = HID // P
HALF = 512
NB = HID // HALF
EXPERTS = 8
RANK = 16
ER = EXPERTS * RANK
AG = ER + EXPERTS
LORA_SCALING = 32.0 / 16.0
LN_EPS = 1e-5
X_SCALE_EXP = 8
W_SCALE_EXP = 14
A_SCALE_EXP = 14
SCORE_SCALE = 1.0 / float(HD) ** 0.5

ALU = mybir.AluOpType
ACT = mybir.ActivationFunctionType
AX = mybir.AxisListType
F32 = mybir.dt.float32
F16 = mybir.dt.float16
I32 = mybir.dt.int32
U32 = mybir.dt.uint32
RMAX = bass.bass_isa.ReduceOp.max

GROUPS = ("k", "q", "v", "base")
MATRICES = ("ag", "k", "q", "v", "base")
AG_, K_, Q_, V_, BASE_ = range(len(MATRICES))


def block_kernel(nc, x, wT, agT, lora_b, biases, out):
    T = x.shape[0] // P
    with ExitStack() as ctx:
        def sb(name, shape, dt=F32):
            return ctx.enter_context(nc.sbuf_tensor(name, shape, dt))

        def ps(name, shape, dt=F32):
            return ctx.enter_context(nc.psum_tensor(name, shape, dt))

        def sem(name):
            return ctx.enter_context(nc.semaphore(name))

        w_hi = {g: sb(f"w_hi_{g}", [P, KC, HID], F16) for g in ("k", "q")}
        w_lo = {g: sb(f"w_lo_{g}", [P, KC, HID], F16) for g in ("k", "q")}
        v_parts = sb("v_parts", [P, 2, KC, HID], F16)
        base_parts = sb("base_parts", [P, KC, 2, HID], F16)
        w_hi["v"], w_lo["v"] = v_parts[:, 0, :, :], v_parts[:, 1, :, :]
        w_hi["base"], w_lo["base"] = base_parts[:, :, 0, :], base_parts[:, :, 1, :]
        ag_hi = sb("ag_hi", [P, KC, AG], F16)
        ag_lo = sb("ag_lo", [P, KC, AG], F16)
        lora_up = sb("lora_up", [P, HID])
        biases_sb = sb("biases_sb", [P, len(GROUPS), HID])
        bias = {g: biases_sb[:, b, :] for b, g in enumerate(GROUPS)}
        ident = sb("ident", [P, P])
        expert_no = sb("expert_no", [P, EXPERTS])
        eps = sb("eps", [P, 1])
        pow_half = sb("pow_half", [P, 1])
        x_scale = sb("x_scale", [P, 1])
        NG = len(MATRICES)
        w_chunk_sum = sb("w_chunk_sum", [P, NG, KC])
        w_part_max = sb("w_part_max", [P, NG])
        w_max = sb("w_max", [P, NG])
        w_clamped = sb("w_clamped", [P, NG])
        w_exp = sb("w_exp", [P, NG], I32)
        w_scale_bits = sb("w_scale_bits", [P, NG], I32)
        w_undo_bits = sb("w_undo_bits", [P, NG], I32)
        w_scale = w_scale_bits[:, :].bitcast(F32)
        w_undo = w_undo_bits[:, :].bitcast(F32)
        a_bias_sum = sb("a_bias_sum", [P, 3])
        a_bound = sb("a_bound", [P, 3])
        a_clamped = sb("a_clamped", [P, 3])
        a_exp = sb("a_exp", [P, 3], I32)
        a_scale_bits = sb("a_scale_bits", [P, 3], I32)
        a_undo_bits = sb("a_undo_bits", [P, 3], I32)
        a_scale = a_scale_bits[:, :].bitcast(F32)
        a_undo = a_undo_bits[:, :].bitcast(F32)
        acc_to_a = sb("acc_to_a", [P, 3])
        score_undo0 = sb("score_undo0", [P, 1])
        score_undo = sb("score_undo", [P, 1])
        ctx_undo = sb("ctx_undo", [P, 1])
        lora_scale0 = sb("lora_scale0", [P, 1])
        lora_scale = sb("lora_scale", [P, 1])

        block_diag_len = QD * P
        work = sb("work", [P, block_diag_len + 10 * HID])
        at = [0]

        def carve(n):
            at[0] += n
            return work[:, at[0] - n:at[0]]

        stage = work[:, 0:KC * HID].rearrange("p (k n) -> p k n", k=KC)
        diag = carve(block_diag_len).bitcast(F16).rearrange("p (t a c) -> p t a c", t=QD, a=2)
        soft = carve(HID)
        res = carve(HID)
        x1 = carve(HID)
        y = carve(HID)
        assert at[0] == KC * HID
        ld = carve(HID)
        xn = carve(HID)
        ev = carve(HID)
        k_parts = carve(HID).bitcast(F16).rearrange("p (t a c) -> p t a c", t=QD, a=2)
        turned = carve(HID)
        parts = carve(HID).bitcast(F16).rearrange("p (t a c) -> p t a c", t=QD, a=2)
        ag_stage = work[:, at[0] - 3 * HID:at[0] - 3 * HID + KC * AG].rearrange("p (k n) -> p k n", k=KC)
        assert KC * AG <= 2 * HID
        q_stage = v_parts[:, :, :, :].rearrange("p a k n -> p (a k n)").bitcast(F32).rearrange(
            "p (k n) -> p k n", k=KC)
        base_slots = base_parts[:, :, :, :].rearrange("p k a n -> p (k a n)").bitcast(F32).rearrange(
            "p (k n) -> p k n", k=KC)
        HK = KC // 2
        SHIFT = 3
        staged = {"k": [stage[:, k, :] for k in range(KC)],
                  "ag": [ag_stage[:, k, :] for k in range(KC)],
                  "q": [q_stage[:, k, :] for k in range(KC)],
                  "v": [stage[:, k, :] for k in range(KC)],
                  "base": [base_slots[:, SHIFT + k, :] if k < KC - SHIFT else stage[:, k, :] for k in range(KC)]}
        order = {g: [*range(KC)] if g in ("ag", "base") else [*range(HK, KC), *range(HK)] for g in MATRICES}
        lo_top = sb("lo_top", [P, 1])
        lo_flag = sb("lo_flag", [P, 1])
        lo_flag_all = sb("lo_flag_all", [P, 1])
        lo_flag_int = sb("lo_flag_int", [P, 1], I32)
        x_hi = sb("x_hi", [P, KC, P], F16)
        x_lo = sb("x_lo", [P, KC, P], F16)
        x2_hi = sb("x2_hi", [P, KC, P], F16)
        x2_lo = sb("x2_lo", [P, KC, P], F16)
        low = sb("low", [P, ER])
        low_t = sb("low_t", [P, P])
        stats = sb("stats", [P, 2, 2, 6])
        mv = sb("mv", [P, 2, 2])
        var = sb("var", [P, 2])
        root_var = sb("root_var", [P, 2])
        rstd = sb("rstd", [P, 2])
        top = sb("top", [P, QD])
        den = sb("den", [P, QD])
        inv = sb("inv", [P, QD])
        logits = sb("logits", [P, EXPERTS])
        best = sb("best", [P, 8])
        best_at = sb("best_at", [P, 8], U32)
        best_no = sb("best_no", [P, 8])
        gap = sb("gap", [P, 1])
        e2 = sb("e2", [P, 1])
        e_sum = sb("e_sum", [P, 1])
        w1 = sb("w1", [P, 1])
        w2 = sb("w2", [P, 1])
        hot1 = sb("hot1", [P, EXPERTS])
        hot2 = sb("hot2", [P, EXPERTS])
        w_full = sb("w_full", [P, EXPERTS])

        acc = [ps(f"acc{i}", [P, HALF]) for i in range(3)]
        turn_ps = ps("turn_ps", [P, HID])
        attn_ps = ps("attn_ps", [P, HID])
        low_ps = ps("low_ps", [P, HALF])

        w_loaded = {g: [sem(f"w_{g}_loaded{k}") for k in range(KC)] for g in GROUPS}
        ag_loaded = sem("ag_loaded")
        const_loaded = sem("const_loaded")
        ident_zero = sem("ident_zero")
        consts_set = sem("consts_set")
        sum_chunk = sem("sum_chunk")
        max_part = sem("max_part")
        max_all = sem("max_all")
        scale_step = sem("scale_step")
        scale_ready = sem("scale_ready")
        undo_ready = sem("undo_ready")
        w_hi_act = sem("w_hi_act")
        w_hi_dve = sem("w_hi_dve")
        bias_summed = sem("bias_summed")
        a_step = sem("a_step")
        bias_scaled = sem("bias_scaled")
        lo_squared = sem("lo_squared")
        lo_step = sem("lo_step")
        lo_flagged = sem("lo_flagged")
        lo_reduced = sem("lo_reduced")
        flag_ready = sem("flag_ready")
        w_lo_done = sem("w_lo_done")
        diag_zero = sem("diag_zero")
        lora_scaled = sem("lora_scaled")

        ld_loaded = sem("ld_loaded")
        res_loaded = sem("res_loaded")
        y_stored = sem("y_stored")
        mv1 = sem("mv1")
        var1 = sem("var1")
        root1 = sem("root1")
        rstd1 = sem("rstd1")
        xn1_ready = sem("xn1_ready")
        xt_done = sem("xt_done")
        xhi_ready = sem("xhi_ready")
        xlo_ready = sem("xlo_ready")
        k_acc = sem("k_acc")
        q_acc = sem("q_acc")
        v_acc = sem("v_acc")
        k_biased = sem("k_biased")
        q_biased = sem("q_biased")
        v_biased = sem("v_biased")
        kt_ready = sem("kt_ready")
        qt_ready = sem("qt_ready")
        vt_ready = sem("vt_ready")
        k_hi_ready = sem("k_hi_ready")
        q_hi_ready = sem("q_hi_ready")
        v_hi_ready = sem("v_hi_ready")
        p_hi_ready = sem("p_hi_ready")
        k_lo_ready = sem("k_lo_ready")
        q_lo_ready = sem("q_lo_ready")
        v_lo_ready = sem("v_lo_ready")
        p_lo_ready = sem("p_lo_ready")
        qdiag_ready = sem("qdiag_ready")
        vdiag_ready = sem("vdiag_ready")
        scored = sem("scored")
        top_ready = sem("top_ready")
        shifted = sem("shifted")
        exped = sem("exped")
        den_ready = sem("den_ready")
        inv_ready = sem("inv_ready")
        prob_ready = sem("prob_ready")
        pt_ready = sem("pt_ready")
        ctx_acc = sem("ctx_acc")
        ctx_turned = sem("ctx_turned")
        x1_ready = sem("x1_ready")
        mv2 = sem("mv2")
        var2 = sem("var2")
        root2 = sem("root2")
        rstd2 = sem("rstd2")
        xn2_ready = sem("xn2_ready")
        x1_biased = sem("x1_biased")
        x2t_done = sem("x2t_done")
        x2hi_ready = sem("x2hi_ready")
        x2lo_ready = sem("x2lo_ready")
        ag_acc = sem("ag_acc")
        best_ready = sem("best_ready")
        best_found = sem("best_found")
        gap_ready = sem("gap_ready")
        e2_ready = sem("e2_ready")
        no_ready = sem("no_ready")
        e_summed = sem("e_summed")
        w1_ready = sem("w1_ready")
        w2_ready = sem("w2_ready")
        hots_ready = sem("hots_ready")
        full_ready = sem("full_ready")
        low_ready = sem("low_ready")
        low_turned = sem("low_turned")
        lowt_ready = sem("lowt_ready")
        base_acc = sem("base_acc")
        base_free = sem("base_free")

        block = ctx.enter_context(nc.Block())
        Q_ACT, Q_DVE = (0,), (1, 2, 3)
        V_ACT, V_DVE = (0, 1), (2, 3)
        turned3 = turned.rearrange("p (t c) -> p t c", t=QD)

        def spread_quadrant(copy, g, ready):
            s = slice(g * QD, (g + 1) * QD)
            copy(diag[s, :, :, s], parts[s, :, :, :]).then_inc(ready, 1)

        A_STEPS = 9
        act_hi = {"ag": 6, "k": 6, "q": 6, "v": KC, "base": KC}
        act_before = {g: sum(act_hi[m] for m in MATRICES[:j]) for j, g in enumerate(MATRICES)}
        n_split = NG * KC

        def rows(ap, t):
            return ap[bass.ds(t * P, P), :]

        def pipeline(eng, step, tail):
            step(0, prev=False, nxt=True)
            with eng.Fori(1, T - 1) as t:
                step(t, prev=True, nxt=True)
            step(T - 1, prev=True, nxt=False)
            tail(T)

        @block.sync
        def _(sp):
            sp.dma_start(ld, rows(x, 0)).then_inc(ld_loaded, 16)

            def load(g):
                src = wT[GROUPS.index(g)]
                for k in order[g]:
                    if g == "v":
                        sp.wait_ge(w_lo_done, K_ * KC + order["k"].index(k) + 1)
                    elif g == "base" and k >= KC - SHIFT:
                        sp.wait_ge(w_lo_done, V_ * KC + order["v"].index(k) + 1)
                    sp.dma_start(staged[g][k], src[k * P:(k + 1) * P, :]).then_inc(w_loaded[g][k], 16)

            sp.dma_start(ag_stage, agT.rearrange("(k p) n -> p k n", p=P)).then_inc(ag_loaded, 16)
            load("k")
            load("q")
            for b, g in enumerate(GROUPS):
                sp.dma_start(bias[g][:, :], biases[b:b + 1, :].to_broadcast([P, HID])).then_inc(const_loaded, 16)
            sp.dma_start(lora_up[:, :], lora_b).then_inc(const_loaded, 16)
            sp.wait_ge(xn1_ready, 1)
            sp.dma_start(ld, rows(x, 1)).then_inc(ld_loaded, 16)
            load("v")
            load("base")
            sp.wait_ge(w_lo_done, n_split)
            sp.dma_start(res, rows(x, 0)).then_inc(res_loaded, 16)

            def store(p):
                sp.wait_ge(base_free, 2 * p + 4)
                sp.dma_start(rows(out, p), y).then_inc(y_stored, 16)

            def step(t, prev, nxt):
                if prev and nxt:
                    sp.wait_ge(xn1_ready, t + 1)
                    sp.dma_start(ld, rows(x, t + 1)).then_inc(ld_loaded, 16)
                if prev:
                    sp.wait_ge(x1_ready, t)
                    sp.dma_start(res, rows(x, t)).then_inc(res_loaded, 16)
                    store(t - 1)

            pipeline(sp, step, lambda t: store(t - 1))
            sp.wait_ge(y_stored, 16 * (T + 1))

        @block.gpsimd
        def _(pool):
            def root(t, i, mv_ready, var_ready, root_ready, rstd_ready):
                pool.wait_ge(mv_ready, t + 1)
                nc.gpsimd.tensor_tensor(var[:, i:i + 1], mv[:, i, 1:2], eps[:, :], ALU.add).then_inc(var_ready, 1)
                pool.wait_ge(var_ready, t + 1)
                nc.gpsimd.tensor_tensor(root_var[:, i:i + 1], var[:, i:i + 1], pow_half[:, :],
                                        ALU.pow).then_inc(root_ready, 1)
                pool.wait_ge(root_ready, t + 1)
                nc.gpsimd.tensor_tensor(rstd[:, i:i + 1], root_var[:, i:i + 1], x_scale[:, :],
                                        ALU.mult).then_inc(rstd_ready, 1)

            nc.gpsimd.memset(ident[:, :], 0.0).then_inc(ident_zero, 1)
            pool.wait_ge(ident_zero, 1)
            nc.gpsimd.affine_select(out=ident[:, :], in_=ident[:, :], compare_op=ALU.not_equal, fill=1.0, base=0,
                                    pattern=[[-1, P]], channel_multiplier=1).then_inc(consts_set, 1)
            for e in range(EXPERTS):
                nc.gpsimd.memset(expert_no[:, e:e + 1], float(e)).then_inc(consts_set, 1)
            nc.gpsimd.memset(eps[:, :], LN_EPS).then_inc(consts_set, 1)
            nc.gpsimd.memset(pow_half[:, :], -0.5).then_inc(consts_set, 1)
            nc.gpsimd.memset(x_scale[:, :], 2.0 ** X_SCALE_EXP).then_inc(consts_set, 1)
            pool.wait_ge(consts_set, EXPERTS + 4)
            root(0, 0, mv1, var1, root1, rstd1)

            def k_low_part(t):
                pool.wait_ge(k_hi_ready, t + 1)
                nc.gpsimd.tensor_tensor(k_parts[:, :, 1, :], turned3, k_parts[:, :, 0, :],
                                        ALU.subtract).then_inc(k_lo_ready, 1)

            def matrix_max(j):
                pool.wait_ge(max_part, j + 1)
                nc.gpsimd.partition_all_reduce(w_max[:, j:j + 1], w_part_max[:, j:j + 1], P, RMAX).then_inc(max_all, 1)

            for j in range(BASE_):
                matrix_max(j)
            pool.wait_ge(xn1_ready, 1)
            root(1, 0, mv1, var1, root1, rstd1)
            k_low_part(0)
            pool.drain()
            pool.wait_ge(w_lo_done, BASE_ * KC)
            nc.gpsimd.memset(work[:, 0:block_diag_len], 0.0).then_inc(diag_zero, 1)
            pool.wait_ge(const_loaded, 16 * (len(GROUPS) + 1))

            def norm2(p):
                root(p, 1, mv2, var2, root2, rstd2)

            def base_bias(p):
                pool.wait_ge(xn2_ready, p + 1)
                nc.gpsimd.tensor_tensor(x1, x1, bias["base"][:, :], ALU.add).then_inc(x1_biased, 1)

            def step(t, prev, nxt):
                if prev and nxt:
                    pool.wait_ge(xn1_ready, t + 1)
                    root(t + 1, 0, mv1, var1, root1, rstd1)
                if prev:
                    pool.wait_ge(scored, t)
                    k_low_part(t)
                    norm2(t - 1)
                    base_bias(t - 1)
                else:
                    pool.wait_ge(lo_flagged, 1)
                    nc.gpsimd.partition_all_reduce(lo_flag_all[:, :], lo_flag[:, :], P, RMAX).then_inc(lo_reduced, 1)
                    matrix_max(BASE_)

            def tail(t):
                norm2(t - 1)
                base_bias(t - 1)

            pipeline(pool, step, tail)

        @block.scalar
        def _(act):
            magnitudes = [part[:, :, :].rearrange("p k n -> p (k n)") for part in (x2_hi, x2_lo)]

            def sums(g):
                j = MATRICES.index(g)
                for i, k in enumerate(order[g]):
                    if g == "ag":
                        act.wait_ge(ag_loaded, 16)
                    else:
                        act.wait_ge(w_loaded[g][k], 16)
                    n = j * KC + i
                    if n >= 2:
                        act.wait_ge(sum_chunk, n - 1)
                    nc.scalar.activation(magnitudes[n % 2][:, 0:staged[g][k].shape[-1]], staged[g][k], ACT.Abs,
                                         accum_out=w_chunk_sum[:, j, k:k + 1]).then_inc(sum_chunk, 1)

            def high_parts(g, hi):
                j = MATRICES.index(g)
                act.wait_ge(scale_ready, j + 1)
                for k in order[g][:act_hi[g]]:
                    if g == "base" and k >= SHIFT:
                        act.wait_ge(w_lo_done, BASE_ * KC + k - SHIFT + 1)
                    nc.scalar.activation(hi[:, k, :], staged[g][k], ACT.Copy,
                                         scale=w_scale[:, j:j + 1]).then_inc(w_hi_act, 1)

            def rows_hi(t, dst, done, ready):
                for h in range(2):
                    act.wait_ge(done, 2 * t + h + 1)
                    c = KC // 2
                    nc.scalar.copy(dst[:, h * c:(h + 1) * c, :],
                                   turn_ps[:, h * HALF:(h + 1) * HALF].rearrange("p (k n) -> p k n", k=c)
                                   ).then_inc(ready, 1)

            rows_hi(0, x_hi, xt_done, xhi_ready)
            sums("ag")
            sums("k")
            high_parts("ag", ag_hi)
            high_parts("k", w_hi["k"])
            sums("q")
            high_parts("q", w_hi["q"])
            sums("v")
            act.wait_ge(const_loaded, 16 * (len(GROUPS) + 1))
            for i in range(3):
                nc.scalar.activation(ev, biases_sb[:, i, :], ACT.Abs,
                                     accum_out=a_bias_sum[:, i:i + 1]).then_inc(bias_summed, 1)
                act.wait_ge(bias_summed, i + 1)
            act.wait_ge(a_step, A_STEPS)
            for i in range(3):
                nc.scalar.activation(biases_sb[:, i, :], biases_sb[:, i, :], ACT.Copy,
                                     scale=a_scale[:, i:i + 1]).then_inc(bias_scaled, 1)
            high_parts("v", w_hi["v"])

            def k_high_part(t):
                act.wait_ge(kt_ready, t + 1)
                nc.scalar.copy(k_parts[:, :, 0, :], turned3).then_inc(k_hi_ready, 1)

            k_high_part(0)
            sums("base")

            def gate_exp(p):
                act.wait_ge(gap_ready, p + 1)
                nc.scalar.activation(e2[:, :], gap[:, :], ACT.Exp).then_inc(e2_ready, 1)

            def low_copy(p):
                act.wait_ge(low_turned, p + 1)
                nc.scalar.copy(low_t[:, :], low_ps[:, 0:P]).then_inc(lowt_ready, 1)

            def step(t, prev, nxt):
                if prev:
                    act.wait_ge(scored, t)
                    k_high_part(t)
                    rows_hi(t - 1, x2_hi, x2t_done, x2hi_ready)
                act.wait_ge(qt_ready, t + 1)
                if prev:
                    act.wait_ge(ctx_acc, t)
                nc.scalar.copy(parts[:, :, 0, :], turned3).then_inc(q_hi_ready, 1)
                if not prev:
                    act.wait_ge(diag_zero, 1)
                act.wait_ge(q_lo_ready, t + 1)
                for g in Q_ACT:
                    spread_quadrant(nc.scalar.copy, g, qdiag_ready)
                if nxt:
                    act.wait_ge(v_acc, 2 * t + 2)
                    rows_hi(t + 1, x_hi, xt_done, xhi_ready)
                act.wait_ge(vt_ready, t + 1)
                act.wait_ge(qdiag_ready, NQ * (t + 1))
                nc.scalar.copy(parts[:, :, 0, :], turned3).then_inc(v_hi_ready, 1)
                if prev:
                    gate_exp(t - 1)
                act.wait_ge(v_lo_ready, t + 1)
                act.wait_ge(scored, t + 1)
                spread_quadrant(nc.scalar.copy, V_ACT[0], vdiag_ready)
                act.wait_ge(shifted, t + 1)
                nc.scalar.activation(soft, soft, ACT.Exp, scale=score_undo[:, 0:1]).then_inc(exped, 1)
                if prev:
                    low_copy(t - 1)
                spread_quadrant(nc.scalar.copy, V_ACT[1], vdiag_ready)
                act.wait_ge(pt_ready, t + 1)
                act.wait_ge(vdiag_ready, NQ * (t + 1))
                nc.scalar.copy(parts[:, :, 0, :], turned3).then_inc(p_hi_ready, 1)
                if not prev:
                    high_parts("base", w_hi["base"])

            def tail(t):
                rows_hi(t - 1, x2_hi, x2t_done, x2hi_ready)
                gate_exp(t - 1)
                low_copy(t - 1)

            pipeline(act, step, tail)

        @block.vector
        def _(dve):
            nc.vector.memset(low[:, :], 0.0).then_inc(base_free, 2)
            nc.vector.memset(logits[:, :], 0.0).then_inc(y_stored, 16)

            def scale(g):
                j = MATRICES.index(g)
                dve.wait_ge(sum_chunk, KC * (j + 1))
                nc.vector.tensor_reduce(w_part_max[:, j:j + 1], w_chunk_sum[:, j, :], AX.X,
                                        ALU.max).then_inc(max_part, 1)
                dve.wait_ge(max_all, j + 1)
                nc.vector.tensor_scalar(w_clamped[:, j:j + 1], w_max[:, j:j + 1], 2.0 ** -90, None,
                                        ALU.max).then_inc(scale_step, 1)
                dve.wait_ge(scale_step, 2 * j + 1)
                nc.vector.tensor_single_scalar(w_exp[:, j:j + 1], w_clamped[:, j:j + 1].bitcast(I32), 0x7F800000,
                                               ALU.bitwise_and).then_inc(scale_step, 1)
                dve.wait_ge(scale_step, 2 * j + 2)
                nc.vector.tensor_scalar(w_scale_bits[:, j:j + 1], w_exp[:, j:j + 1], -1.0,
                                        float((W_SCALE_EXP + 254) << 23), ALU.mult, ALU.add).then_inc(scale_ready, 1)
                nc.vector.tensor_scalar(w_undo_bits[:, j:j + 1], w_exp[:, j:j + 1],
                                        float((W_SCALE_EXP + X_SCALE_EXP) << 23), None, ALU.subtract
                                        ).then_inc(undo_ready, 1)

            def split(g, hi, lo):
                j = MATRICES.index(g)
                dve.wait_ge(scale_ready, j + 1)
                if g == "v":
                    dve.wait_ge(w_lo_done, V_ * KC)
                for i, k in enumerate(order[g]):
                    if g == "base" and k >= SHIFT:
                        dve.wait_ge(w_lo_done, BASE_ * KC + k - SHIFT + 1)
                    if i < act_hi[g]:
                        dve.wait_ge(w_hi_act, act_before[g] + i + 1)
                    else:
                        nc.vector.tensor_scalar(hi[:, k, :], staged[g][k], w_scale[:, j:j + 1], None,
                                                ALU.mult).then_inc(w_hi_dve, 1)
                        dve.wait_ge(w_hi_dve, j * KC - act_before[g] + i - act_hi[g] + 1)
                    nc.vector.scalar_tensor_tensor(out=lo[:, k, :], in0=staged[g][k],
                                                   scalar=w_scale[:, j:j + 1], in1=hi[:, k, :], op0=ALU.mult,
                                                   op1=ALU.subtract).then_inc(w_lo_done, 1)

            def lora_scaling():
                nc.vector.tensor_tensor(lora_scale0[:, :], w_undo[:, AG_:AG_ + 1], w_scale[:, BASE_:BASE_ + 1],
                                        ALU.mult).then_inc(lora_scaled, 1)
                dve.wait_ge(lora_scaled, 1)
                nc.vector.tensor_scalar(lora_scale[:, :], lora_scale0[:, :], 2.0 ** X_SCALE_EXP * LORA_SCALING,
                                        None, ALU.mult).then_inc(lora_scaled, 1)
                dve.wait_ge(lora_scaled, 2)

            def flag_low_parts():
                dve.wait_ge(lo_squared, 1)
                nc.vector.tensor_reduce(lo_top[:, :], low_ps[:, 0:P], AX.X, ALU.max,
                                        apply_absolute_value=True).then_inc(lo_step, 1)
                dve.wait_ge(lo_step, 1)
                nc.vector.tensor_scalar(lo_flag[:, :], lo_top[:, :], 0.0, None, ALU.not_equal).then_inc(lo_flagged, 1)

            def publish_flag():
                dve.wait_ge(lo_reduced, 1)
                nc.vector.tensor_copy(lo_flag_int[:, :], lo_flag_all[:, :]).then_inc(flag_ready, 1)

            def ln_stats(i, src, mean_ready):
                for h in range(2):
                    nc.vector.bn_stats(stats[:, i, h, :], src[:, h * HALF:(h + 1) * HALF])
                dve.drain()
                nc.vector.bn_aggr(mv[:, i, :], stats[:, i, :, :].rearrange("p a b -> p (a b)")).then_inc(mean_ready, 1)

            def normalise(t, i, src, rstd_ready, ready):
                dve.wait_ge(rstd_ready, t + 1)
                nc.vector.tensor_scalar(xn, src, mv[:, i, 0:1], rstd[:, i:i + 1], ALU.subtract,
                                        ALU.mult).then_inc(ready, 1)

            def rows_lo(t, dst, hi, hi_ready, ready):
                c = KC // 2
                for h in range(2):
                    dve.wait_ge(hi_ready, 2 * t + h + 1)
                    nc.vector.tensor_tensor(dst[:, h * c:(h + 1) * c, :],
                                            turn_ps[:, h * HALF:(h + 1) * HALF].rearrange("p (k n) -> p k n", k=c),
                                            hi[:, h * c:(h + 1) * c, :], ALU.subtract).then_inc(ready, 1)

            a_steps = [0]

            def a_next(instruction):
                instruction.then_inc(a_step, 1)
                a_steps[0] += 1
                dve.wait_ge(a_step, a_steps[0])

            def attention_scales():
                dve.wait_ge(bias_summed, 3)
                a_next(nc.vector.scalar_tensor_tensor(out=a_bound[:, :], in0=w_max[:, K_:V_ + 1], scalar=float(HID),
                                                      in1=a_bias_sum[:, :], op0=ALU.mult, op1=ALU.add))
                a_next(nc.vector.tensor_scalar(a_clamped[:, :], a_bound[:, :], 2.0 ** -90, None, ALU.max))
                a_next(nc.vector.tensor_single_scalar(a_exp[:, :], a_clamped[:, :].bitcast(I32), 0x7F800000,
                                                      ALU.bitwise_and))
                a_next(nc.vector.tensor_scalar(a_scale_bits[:, :], a_exp[:, :], -1.0,
                                               float((A_SCALE_EXP + 254) << 23), ALU.mult, ALU.add))
                a_next(nc.vector.tensor_scalar(a_undo_bits[:, :], a_exp[:, :], float(A_SCALE_EXP << 23), None,
                                               ALU.subtract))
                dve.wait_ge(undo_ready, V_ + 1)
                a_next(nc.vector.tensor_tensor(acc_to_a[:, :], w_undo[:, K_:V_ + 1], a_scale, ALU.mult))
                a_next(nc.vector.tensor_tensor(score_undo0[:, :], a_undo[:, 0:1], a_undo[:, 1:2], ALU.mult))
                a_next(nc.vector.tensor_scalar(score_undo[:, :], score_undo0[:, :], SCORE_SCALE, None, ALU.mult))
                a_next(nc.vector.tensor_scalar(ctx_undo[:, :], a_undo[:, 2:3], 2.0 ** -A_SCALE_EXP, None, ALU.mult))
                assert a_steps[0] == A_STEPS

            def low_part(t, hi_ready, lo_ready):
                dve.wait_ge(hi_ready, t + 1)
                nc.vector.tensor_tensor(parts[:, :, 1, :], turned3, parts[:, :, 0, :],
                                        ALU.subtract).then_inc(lo_ready, 1)

            def add_bias(t, n, g, i, bank, acc_done, biased):
                dve.wait_ge(acc_done, 2 * t + n + 1)
                s = slice(n * HALF, (n + 1) * HALF)
                nc.vector.scalar_tensor_tensor(out=ev[:, s], in0=acc[bank][:, :], scalar=acc_to_a[:, i:i + 1],
                                               in1=bias[g][:, s], op0=ALU.mult, op1=ALU.add).then_inc(biased, 1)

            ev_heads = ev.rearrange("p (h d) -> p h d", h=HEADS)

            dve.wait_ge(ld_loaded, 16)
            ln_stats(0, ld, mv1)
            normalise(0, 0, ld, rstd1, xn1_ready)
            rows_lo(0, x_lo, x_hi, xhi_ready, xlo_ready)
            scale("ag")
            scale("k")
            split("ag", ag_hi, ag_lo)
            split("k", w_hi["k"], w_lo["k"])
            scale("q")
            split("q", w_hi["q"], w_lo["q"])
            scale("v")
            attention_scales()
            dve.wait_ge(const_loaded, 16 * (len(GROUPS) + 1))
            dve.wait_ge(consts_set, EXPERTS + 4)

            def gating(p):
                dve.wait_ge(ag_acc, p + 1)
                nc.vector.tensor_scalar(logits[:, :], acc[0][:, ER:AG], w_undo[:, AG_:AG_ + 1], None,
                                        ALU.mult)
                dve.drain()
                nc.vector.max(best[:, :], logits[:, :]).then_inc(best_ready, 1)
                dve.wait_ge(best_ready, p + 1)
                nc.vector.tensor_tensor(gap[:, :], best[:, 1:2], best[:, 0:1], ALU.subtract).then_inc(gap_ready, 1)
                nc.vector.max_index(best_at[:, :], best[:, :], logits[:, :]).then_inc(best_found, 1)
                dve.wait_ge(best_found, p + 1)
                nc.vector.tensor_copy(best_no[:, :], best_at[:, :]).then_inc(no_ready, 1)
                dve.wait_ge(e2_ready, p + 1)
                nc.vector.tensor_scalar(e_sum[:, :], e2[:, :], 1.0, None, ALU.add).then_inc(e_summed, 1)
                dve.wait_ge(e_summed, p + 1)
                nc.vector.reciprocal(w1[:, :], e_sum[:, :]).then_inc(w1_ready, 1)
                dve.wait_ge(w1_ready, p + 1)
                nc.vector.tensor_tensor(w2[:, :], e2[:, :], w1[:, :], ALU.mult).then_inc(w2_ready, 1)
                dve.wait_ge(no_ready, p + 1)
                nc.vector.tensor_scalar(hot1[:, :], expert_no[:, :], best_no[:, 0:1], w1[:, 0:1], ALU.is_equal,
                                        ALU.mult).then_inc(hots_ready, 1)
                dve.wait_ge(w2_ready, p + 1)
                nc.vector.tensor_scalar(hot2[:, :], expert_no[:, :], best_no[:, 1:2], w2[:, 0:1], ALU.is_equal,
                                        ALU.mult).then_inc(hots_ready, 1)
                dve.wait_ge(hots_ready, 2 * p + 2)
                nc.vector.tensor_tensor(w_full[:, :], hot1[:, :], hot2[:, :], ALU.add).then_inc(full_ready, 1)
                dve.wait_ge(full_ready, p + 1)
                nc.vector.scalar_tensor_tensor(
                    out=low[:, :].rearrange("p (e r) -> p e r", e=EXPERTS),
                    in0=acc[0][:, 0:ER].rearrange("p (e r) -> p e r", e=EXPERTS), scalar=lora_scale[:, 0:1],
                    in1=w_full[:, :].unsqueeze(2).to_broadcast([P, EXPERTS, RANK]),
                    op0=ALU.mult, op1=ALU.mult).then_inc(low_ready, 1)

            def finish(p, n):
                s = slice(n * HALF, (n + 1) * HALF)
                if n == 0:
                    dve.wait_ge(x1_biased, p + 1)
                    dve.wait_ge(y_stored, 16 * (p + 1))
                dve.wait_ge(base_acc, 2 * p + n + 1)
                nc.vector.scalar_tensor_tensor(out=y[:, s], in0=acc[1 + n][:, :], scalar=w_undo[:, BASE_:BASE_ + 1],
                                               in1=x1[:, s], op0=ALU.mult, op1=ALU.add).then_inc(base_free, 1)

            def attention_end(p):
                dve.wait_ge(ctx_acc, p + 1)
                nc.vector.transpose(ev_heads, attn_ps[:, :].rearrange("p (t h) -> p h t", t=QD)
                                    ).then_inc(ctx_turned, 1)
                dve.wait_ge(ctx_turned, p + 1)
                dve.wait_ge(res_loaded, 16 * (p + 1))
                dve.wait_ge(base_free, 2 * p + 2)
                nc.vector.scalar_tensor_tensor(out=x1, in0=ev, scalar=ctx_undo[:, 0:1], in1=res, op0=ALU.mult,
                                               op1=ALU.add).then_inc(x1_ready, 1)
                dve.wait_ge(x1_ready, p + 1)

            def norm2(p):
                dve.wait_ge(xt_done, 2 * p + 2)
                normalise(p, 1, x1, rstd2, xn2_ready)

            def take_k(t, prev, nxt):
                add_bias(t, 0, "k", 0, 0, k_acc, k_biased)
                if nxt:
                    dve.wait_ge(ld_loaded, 16 * (t + 2))
                    ln_stats(0, ld, mv1)
                add_bias(t, 1, "k", 0, 1, k_acc, k_biased)
                dve.wait_ge(k_biased, 2 * t + 2)
                if prev:
                    dve.wait_ge(p_lo_ready, t)
                nc.vector.transpose(turned.rearrange("p (t h) -> p h t", t=QD), ev_heads).then_inc(kt_ready, 1)

            def first_k():
                dve.wait_ge(bias_scaled, 3)
                take_k(0, prev=False, nxt=True)

            def step(t, prev, nxt):
                if prev:
                    take_k(t, prev, nxt)
                dve.wait_ge(kt_ready, t + 1)
                if prev:
                    attention_end(t - 1)
                    ln_stats(1, x1, mv2)
                add_bias(t, 0, "q", 1, 2, q_acc, q_biased)
                add_bias(t, 1, "q", 1, 0, q_acc, q_biased)
                if prev:
                    norm2(t - 1)
                dve.wait_ge(q_biased, 2 * t + 2)
                dve.wait_ge(k_lo_ready, t + 1)
                nc.vector.transpose(turned.rearrange("p (t h) -> p h t", t=QD), ev_heads).then_inc(qt_ready, 1)
                if prev:
                    dve.wait_ge(qt_ready, t + 1)
                    add_bias(t, 0, "v", 2, 1, v_acc, v_biased)
                    rows_lo(t - 1, x2_lo, x2_hi, x2hi_ready, x2lo_ready)
                    if nxt:
                        dve.wait_ge(x2t_done, 2 * t)
                        normalise(t + 1, 0, ld, rstd1, xn1_ready)
                low_part(t, q_hi_ready, q_lo_ready)
                if not prev:
                    dve.wait_ge(diag_zero, 1)
                dve.wait_ge(q_lo_ready, t + 1)
                for g in Q_DVE:
                    spread_quadrant(nc.vector.tensor_copy, g, qdiag_ready)
                if not prev:
                    normalise(1, 0, ld, rstd1, xn1_ready)
                    dve.wait_ge(qt_ready, t + 1)
                    add_bias(t, 0, "v", 2, 1, v_acc, v_biased)
                add_bias(t, 1, "v", 2, 2, v_acc, v_biased)
                dve.wait_ge(v_biased, 2 * t + 2)
                dve.wait_ge(q_lo_ready, t + 1)
                dve.wait_ge(qdiag_ready, NQ * (t + 1))
                nc.vector.transpose(turned.rearrange("p (t d) -> p d t", t=QD),
                                    ev.rearrange("p (h d) -> p d h", h=HEADS)).then_inc(vt_ready, 1)
                low_part(t, v_hi_ready, v_lo_ready)
                dve.wait_ge(vt_ready, t + 1)
                if prev:
                    gating(t - 1)
                if nxt:
                    dve.wait_ge(v_acc, 2 * t + 2)
                    rows_lo(t + 1, x_lo, x_hi, xhi_ready, xlo_ready)
                dve.wait_ge(scored, t + 1)
                scores = attn_ps[:, :].rearrange("p (t c) -> p t c", t=QD)
                s3 = soft.rearrange("p (t c) -> p t c", t=QD)
                nc.vector.tensor_reduce(top[:, :], scores, AX.X, ALU.max).then_inc(top_ready, 1)
                dve.wait_ge(top_ready, t + 1)
                nc.vector.tensor_tensor(s3, scores, top[:, :].unsqueeze(2).to_broadcast([P, QD, QD]),
                                        ALU.subtract).then_inc(shifted, 1)
                dve.wait_ge(v_lo_ready, t + 1)
                for g in V_DVE:
                    spread_quadrant(nc.vector.tensor_copy, g, vdiag_ready)
                if not prev:
                    flag_low_parts()
                dve.wait_ge(exped, t + 1)
                nc.vector.tensor_reduce(den[:, :], s3, AX.X, ALU.add).then_inc(den_ready, 1)
                dve.wait_ge(den_ready, t + 1)
                nc.vector.reciprocal(inv[:, :], den[:, :]).then_inc(inv_ready, 1)
                dve.wait_ge(inv_ready, t + 1)
                if not prev:
                    publish_flag()
                nc.vector.scalar_tensor_tensor(out=s3, in0=s3, scalar=2.0 ** A_SCALE_EXP,
                                               in1=inv[:, :].unsqueeze(2).to_broadcast([P, QD, QD]), op0=ALU.mult,
                                               op1=ALU.mult).then_inc(prob_ready, 1)
                dve.wait_ge(prob_ready, t + 1)
                nc.vector.transpose(turned, soft).then_inc(pt_ready, 1)
                if prev:
                    finish(t - 1, 0)
                low_part(t, p_hi_ready, p_lo_ready)
                if prev:
                    finish(t - 1, 1)
                else:
                    scale("base")
                    split("base", w_hi["base"], w_lo["base"])
                    dve.wait_ge(undo_ready, NG)
                    lora_scaling()
                dve.wait_ge(pt_ready, t + 1)

            def tail(t):
                attention_end(t - 1)
                ln_stats(1, x1, mv2)
                norm2(t - 1)
                rows_lo(t - 1, x2_lo, x2_hi, x2hi_ready, x2lo_ready)
                gating(t - 1)
                finish(t - 1, 0)
                finish(t - 1, 1)

            first_k()
            split("v", w_hi["v"], w_lo["v"])
            pipeline(dve, step, tail)

        @block.tensor
        def _(pe):
            pe.wait_ge(consts_set, EXPERTS + 4)

            def turn_rows(t, xn_ready, done):
                pe.wait_ge(xn_ready, t + 1)
                for k in range(KC):
                    mm = nc.tensor.transpose(turn_ps[:, k * P:(k + 1) * P], xn[:, k * P:(k + 1) * P], ident[:, :])
                    if k % (KC // 2) == KC // 2 - 1:
                        mm.then_inc(done, 1)

            def attend_one(moving, i):
                dst = attn_ps[:, i * QD:(i + 1) * QD]
                nc.tensor.matmul(dst, diag[:, i, 0, :], moving[:, i, 0, :], start=True, stop=False)
                nc.tensor.matmul(dst, diag[:, i, 0, :], moving[:, i, 1, :], start=False, stop=False)
                return nc.tensor.matmul(dst, diag[:, i, 1, :], moving[:, i, 0, :], start=False, stop=True)

            def project(t, g, n, bank, done, any_low, moving=None, first=0, attended=None):
                cols = slice(n * HALF, (n + 1) * HALF)
                dst = acc[bank][:, :]
                for k in range(KC):
                    nc.tensor.matmul(dst, x_hi[:, k, :], w_hi[g][:, k, cols], start=(k == 0), stop=False)
                    if moving is not None:
                        attend_one(moving, first + k)
                if any_low is None:
                    for k in range(KC):
                        nc.tensor.matmul(dst, x_hi[:, k, :], w_lo[g][:, k, cols], start=False, stop=False)
                else:
                    with pe.If(any_low > 0):
                        for k in range(KC):
                            nc.tensor.matmul(dst, x_hi[:, k, :], w_lo[g][:, k, cols], start=False, stop=False)
                for k in range(KC):
                    mm = nc.tensor.matmul(dst, x_lo[:, k, :], w_hi[g][:, k, cols], start=False, stop=(k == KC - 1))
                    if k == KC - 1:
                        mm.then_inc(done, 1)
                    if moving is not None:
                        small = attend_one(moving, first + KC + k)
                if attended is not None:
                    small.then_inc(attended, 1)

            def square_low_parts(g):
                for k in range(KC):
                    for c in range(HID // P):
                        part = w_lo[g][:, k, c * P:(c + 1) * P]
                        mm = nc.tensor.matmul(low_ps[:, 0:P], part, part, start=(g == "k" and k == 0 and c == 0),
                                              stop=(g == "v" and k == KC - 1 and c == HID // P - 1))
                if g == "v":
                    mm.then_inc(lo_squared, 1)

            def experts(p):
                pe.wait_ge(x2hi_ready, 2 * p + 2)
                pe.wait_ge(x2lo_ready, 2 * p + 2)
                dst = acc[0][:, 0:AG]
                for k in range(KC):
                    nc.tensor.matmul(dst, x2_hi[:, k, :], ag_hi[:, k, :], start=(k == 0), stop=False)
                    nc.tensor.matmul(dst, x2_hi[:, k, :], ag_lo[:, k, :], start=False, stop=False)
                    mm = nc.tensor.matmul(dst, x2_lo[:, k, :], ag_hi[:, k, :], start=False, stop=(k == KC - 1))
                mm.then_inc(ag_acc, 1)

            def turn_low(p):
                pe.wait_ge(low_ready, p + 1)
                nc.tensor.transpose(low_ps[:, 0:P], low[:, :], ident[:, :]).then_inc(low_turned, 1)

            def dense(n, moving=None):
                cols = slice(n * HALF, (n + 1) * HALF)
                dst = acc[1 + n][:, :]
                parts_of = ((x2_hi, w_hi["base"]), (x2_hi, w_lo["base"]), (x2_lo, w_hi["base"]))
                steps = len(parts_of) * KC
                for m in range(steps):
                    rows_part, w_part = parts_of[m % 3]
                    nc.tensor.matmul(dst, rows_part[:, m // 3, :], w_part[:, m // 3, cols], start=(m == 0),
                                     stop=False)
                    if moving is not None:
                        for i in range(m * QD // steps, (m + 1) * QD // steps):
                            small = attend_one(moving, i)
                if moving is not None:
                    small.then_inc(scored, 1)

            def dense_lora(p):
                pe.wait_ge(lowt_ready, p + 1)
                for n in range(NB):
                    nc.tensor.matmul(acc[1 + n][:, :], low_t[:, :], lora_up[:, n * HALF:(n + 1) * HALF],
                                     start=False, stop=True).then_inc(base_acc, 1)

            def context_ready(p):
                pe.wait_ge(vdiag_ready, NQ * (p + 1))
                pe.wait_ge(p_lo_ready, p + 1)

            turn_rows(0, xn1_ready, xt_done)
            any_low = [None]

            def step(t, prev, nxt):
                pe.wait_ge(xhi_ready, 2 * t + 2)
                pe.wait_ge(xlo_ready, 2 * t + 2)
                if not prev:
                    pe.wait_ge(w_lo_done, (K_ + 1) * KC)
                else:
                    pe.wait_ge(q_biased, 2 * t)
                project(t, "k", 0, 0, k_acc, any_low[0])
                if prev:
                    pe.wait_ge(base_free, 2 * t - 1)
                    context_ready(t - 1)
                project(t, "k", 1, 1, k_acc, any_low[0], moving=parts if prev else None)
                if prev:
                    pe.wait_ge(base_free, 2 * t)
                else:
                    pe.wait_ge(w_lo_done, (Q_ + 1) * KC)
                project(t, "q", 0, 2, q_acc, any_low[0], moving=parts if prev else None, first=2 * KC,
                        attended=ctx_acc if prev else None)
                if not prev:
                    square_low_parts("k")
                    square_low_parts("q")
                pe.wait_ge(k_biased, 2 * t + 2)
                project(t, "q", 1, 0, q_acc, any_low[0])
                if not prev:
                    pe.wait_ge(w_lo_done, (V_ + 1) * KC)
                project(t, "v", 0, 1, v_acc, any_low[0])
                if prev:
                    turn_rows(t - 1, xn2_ready, x2t_done)
                pe.wait_ge(q_biased, 2 * t + 1)
                project(t, "v", 1, 2, v_acc, any_low[0])
                if prev:
                    pe.wait_ge(q_biased, 2 * t + 2)
                    experts(t - 1)
                if nxt:
                    if prev:
                        pe.wait_ge(x2lo_ready, 2 * t)
                    turn_rows(t + 1, xn1_ready, xt_done)
                pe.wait_ge(k_lo_ready, t + 1)
                pe.wait_ge(qdiag_ready, NQ * (t + 1))
                if prev:
                    pe.wait_ge(ctx_turned, t)
                    pe.wait_ge(v_biased, 2 * t + 1)
                    pe.wait_ge(w_lo_done, n_split)
                    if nxt:
                        dense(0, k_parts)
                    else:
                        for i in range(QD):
                            small = attend_one(k_parts, i)
                        small.then_inc(scored, 1)
                        dense(0)
                    turn_low(t - 1)
                    pe.wait_ge(v_biased, 2 * t + 2)
                    dense(1)
                    dense_lora(t - 1)
                else:
                    for i in range(QD):
                        small = attend_one(k_parts, i)
                    small.then_inc(scored, 1)
                    square_low_parts("v")
                    pe.wait_ge(flag_ready, 1)
                    any_low[0] = pe.value_load(lo_flag_int[0:1, 0:1], min_val=0, max_val=1)

            def tail(t):
                context_ready(t - 1)
                for i in range(QD):
                    small = attend_one(parts, i)
                small.then_inc(ctx_acc, 1)
                turn_rows(t - 1, xn2_ready, x2t_done)
                pe.wait_ge(low_ready, t - 1)
                experts(t - 1)
                pe.wait_ge(base_free, 2 * t)
                dense(0)
                turn_low(t - 1)
                dense(1)
                dense_lora(t - 1)

            pipeline(pe, step, tail)


def kernel(**inputs):
    import numpy as np
    import concourse.bacc as bacc
    from concourse.bass_utils import run_bass_kernel_spmd

    def get(name):
        return np.asarray(inputs[name])

    x = get("L0_attn_hidden_states")
    B, S, D = x.shape
    arrays = {
        "x_dram": x.reshape(B * S, D),
        "wT_dram": np.stack([get("L0_attn_wk").T, get("L0_attn_wq").T, get("L0_attn_wv").T,
                             get("L0_ffn_base_w").T]),
        "agT_dram": np.concatenate([get("L0_ffn_lora_A").reshape(ER, D).T, get("L0_ffn_gate_w").T], axis=1),
        "lora_b_dram": get("L0_ffn_lora_B").transpose(0, 2, 1).reshape(ER, D),
        "bias_dram": np.stack([get("L0_attn_bk"), get("L0_attn_bq"), get("L0_attn_bv"), get("L0_ffn_base_b")]),
    }
    arrays = {n: np.ascontiguousarray(a) for n, a in arrays.items()}
    nc = bacc.Bacc("TRN2", target_bir_lowering=False, num_devices=1, dynamic_dma_scratch_size=1024)
    args = [nc.dram_tensor(n, a.shape, mybir.dt.from_np(a.dtype), kind="ExternalInput").ap()
            for n, a in arrays.items()]
    out = nc.dram_tensor("out_dram", (B * S, D), F32, kind="ExternalOutput").ap()
    block_kernel(nc, *args, out)
    r = run_bass_kernel_spmd(nc, [arrays], core_ids=[0])
    return r.results[0]["out_dram"].reshape(B, S, D)
```
